# Optimizing a Trainium2 kernel written in Bass

```python
import numpy as np
import jax
import jax.numpy as jnp

def _softmax(x, axis=-1):
    return jax.nn.softmax(x, axis=axis)

def _gelu(x):
    return jax.nn.gelu(x, approximate=True)

def _silu(x):
    return jax.nn.silu(x)

def _sigmoid(x):
    return jax.nn.sigmoid(x)

def _layernorm(x, axis=-1, eps=1e-05):
    m = jnp.mean(x, axis=axis, keepdims=True)
    v = jnp.var(x, axis=axis, keepdims=True)
    return (x - m) / jnp.sqrt(v + eps)

def _scatter_add(tgt, idx, src, axis=0):
    return tgt.at[idx].add(src)

def _segment_sum(src, seg, n):
    return jax.ops.segment_sum(src, seg, n)
kernel_name = 'mk_seq_postln_d1_jaxref_r8_ff2d49'

def setup_inputs(seed: int=0):
    np.random.seed(seed)
    _w = jnp.asarray

    def _L0_attn_setup():
        import jax, jax.numpy as jnp
        import numpy as np
        B, S, D = (2, 256, 256)
        H, G = (16, 4)
        HD = D // H
        KV = HD * G
        key = jax.random.key(seed)
        ks = jax.random.split(key, 5)
        scale = 1.0 / np.sqrt(D)
        return {'x': jax.random.normal(ks[0], (B, S, D), dtype=jnp.float32), 'Wqkv': jax.random.normal(ks[1], (D, D + 2 * KV), dtype=jnp.float32) * scale, 'bqkv': jax.random.normal(ks[2], (D + 2 * KV,), dtype=jnp.float32) * 0.01, 'Wout': jax.random.normal(ks[3], (D, D), dtype=jnp.float32) * scale, 'bout': jax.random.normal(ks[4], (D,), dtype=jnp.float32) * 0.01}
    _L0_attn_in = _L0_attn_setup()

    def _L0_ffn_setup():
        import jax, jax.numpy as jnp
        import numpy as np
        GROUP_SIZE = 64

        def ternary_quant(w_fp32, g=GROUP_SIZE):
            w = w_fp32.astype(jnp.bfloat16)
            w_g = w.reshape(-1, g)
            scale = jnp.clip(jnp.mean(jnp.abs(w_g), axis=-1, keepdims=True), 1e-08, None)
            q = jnp.clip(jnp.round(w_g / scale), -1, 1)
            w_hat = (q * scale).reshape(w.shape)
            return w + jax.lax.stop_gradient(w_hat - w)

        def rms_norm(x):
            eps = jnp.finfo(x.dtype).eps.astype(jnp.float32)
            xf = x.astype(jnp.float32)
            inv = jax.lax.rsqrt(jnp.mean(xf * xf, axis=-1, keepdims=True) + eps)
            return (xf * inv).astype(x.dtype)
        key = jax.random.key(seed)
        k1, k2, k3 = jax.random.split(key, 3)
        B, S, D = (2, 256, 256)
        H = 4 * D
        x = jax.random.normal(k1, (B, S, D), dtype=jnp.float32).astype(jnp.bfloat16)
        w_gate_up = jax.random.normal(k2, (2 * H, D), dtype=jnp.float32) * 0.02
        w_proj = jax.random.normal(k3, (D, H), dtype=jnp.float32) * 0.02
        return {'x': x, 'w_gate_up': w_gate_up, 'w_proj': w_proj}
    _L0_ffn_in = _L0_ffn_setup()
    _d = {'L0_attn_x': _L0_attn_in['x'], 'L0_attn_Wqkv': _L0_attn_in['Wqkv'], 'L0_attn_bqkv': _L0_attn_in['bqkv'], 'L0_attn_Wout': _L0_attn_in['Wout'], 'L0_attn_bout': _L0_attn_in['bout'], 'L0_ffn_w_gate_up': _L0_ffn_in['w_gate_up'], 'L0_ffn_w_proj': _L0_ffn_in['w_proj']}
    _x0 = _d['L0_attn_x']
    _d['L0_attn_x'] = jax.random.normal(jax.random.fold_in(jax.random.key(seed), 1), (16, 256, 256), dtype=_x0.dtype)
    del _x0
    return _d

def reference(L0_attn_x, L0_attn_Wqkv, L0_attn_bqkv, L0_attn_Wout, L0_attn_bout, L0_ffn_w_gate_up, L0_ffn_w_proj):

    def _L0_attn_ref(x, Wqkv, bqkv, Wout, bout):
        import jax, jax.numpy as jnp
        import numpy as np
        B, S, D = (2, 256, 256)
        H, G = (16, 4)
        HD = D // H
        KV = HD * G
        b, s, _ = x.shape
        qkv = x @ Wqkv + bqkv
        q, k, v = jnp.split(qkv, [D, D + KV], axis=-1)
        q = q.reshape(b, s, H, HD)
        k = jnp.tile(k.reshape(b, s, G, HD), (1, 1, H // G, 1))
        v = jnp.tile(v.reshape(b, s, G, HD), (1, 1, H // G, 1))
        scores = jnp.einsum('bqhd,bkhd->bhqk', q, k) / HD
        prob = jax.nn.softmax(scores, axis=-1)
        out = jnp.einsum('bhqk,bkhd->bqhd', prob, v).reshape(b, s, D)
        return out @ Wout + bout

    def _L0_ffn_ref(x, w_gate_up, w_proj):
        import jax, jax.numpy as jnp
        import numpy as np
        GROUP_SIZE = 64

        def ternary_quant(w_fp32, g=GROUP_SIZE):
            w = w_fp32.astype(jnp.bfloat16)
            w_g = w.reshape(-1, g)
            scale = jnp.clip(jnp.mean(jnp.abs(w_g), axis=-1, keepdims=True), 1e-08, None)
            q = jnp.clip(jnp.round(w_g / scale), -1, 1)
            w_hat = (q * scale).reshape(w.shape)
            return w + jax.lax.stop_gradient(w_hat - w)

        def rms_norm(x):
            eps = jnp.finfo(x.dtype).eps.astype(jnp.float32)
            xf = x.astype(jnp.float32)
            inv = jax.lax.rsqrt(jnp.mean(xf * xf, axis=-1, keepdims=True) + eps)
            return (xf * inv).astype(x.dtype)
        wq_gu = ternary_quant(w_gate_up)
        gu = jnp.einsum('bsd,hd->bsh', x, wq_gu)
        gate, up = jnp.split(gu, 2, axis=-1)
        h = jax.nn.silu(gate) * up
        hn = rms_norm(h)
        wq_p = ternary_quant(w_proj)
        return jnp.einsum('bsh,dh->bsd', hn, wq_p)
    x = L0_attn_x
    x = _layernorm(x + _L0_attn_ref(x, L0_attn_Wqkv, L0_attn_bqkv, L0_attn_Wout, L0_attn_bout), axis=-1)
    x = _layernorm(x + _L0_ffn_ref(x, L0_ffn_w_gate_up, L0_ffn_w_proj), axis=-1)
    return x

_drawn_inputs = setup_inputs


def setup_inputs(seed=0):
    import zlib

    import numpy as np

    out = dict(_drawn_inputs(seed))
    spreads = {}
    factors = {'L0_attn_bqkv': 5.485, 'L0_attn_bout': 5.462}
    for name, (base, spread) in spreads.items():
        noise = np.random.default_rng([zlib.crc32(name.encode()), seed]).standard_normal(out[name].shape)
        drawn = base * np.exp(spread * noise) if base else spread * noise
        out[name] = jnp.asarray(drawn.astype(out[name].dtype))
    for name, factor in factors.items():
        out[name] = (out[name] * factor).astype(out[name].dtype)
    return out
```

```python
from contextlib import ExitStack

import concourse.bass as bass
from concourse import mybir

ALU = mybir.AluOpType
ACT = mybir.ActivationFunctionType
AX = mybir.AxisListType
F32 = mybir.dt.float32
F32R = mybir.dt.float32r
BF16 = mybir.dt.bfloat16

P = 128
B, S, D = 16, 256, 256
H, G, HD = 16, 4, 16
KV = G * HD
F = 4 * D
TT = S // P
DT = D // P
FT = F // P
Q_GROUP = 64
LN_EPS = 1e-5
RMS_EPS = 2.0 ** -23

SLOTS = 8
LOAD_X, X_T, PROJ_Q, PROJ_K, SAVE_QK, STACK_QK, MAX0, PROJ_V = 0, 1, 2, 2, 3, 4, 6, 8
SHIFT_T = (11, 15)
EXP0 = 13
PV0 = EXP0 + 1
PV_COPY = (PV0 + 3, PV0 + 7)
PV_T = (20, 22)
LOAD_RES, ADD_BOUT, ATT_T, PROJ_O, LN1_APPLY, X1_T = 23, 24, 24, 25, 26, 27
FFN0 = 28
DOWN0 = FFN0 + 1
SUM_SQ, LN2_STATS, LN2_APPLY = 37, 38, 39
Y_COPY = DOWN0 + 7
STORE = 39

LAST = SLOTS * B + STORE
LOOP_FROM, BODY = 48, 2 * SLOTS
LOOPS = (SLOTS * B - LOOP_FROM) // BODY


def first_head(c):
    return 8 * (c // 4) + c % 4


def quadrant(g, i):
    return 2 * (g % 2) + i


class Step:

    def __init__(self, b, s, it):
        self.b, self.s, self.it = b, s, it
        self.par = b % 2

    def count(self, per, extra):
        v = per * self.b + extra
        assert self.it is None or v > 0
        return v if self.it is None else self.it * (2 * per) + v

    def count2(self, per, extra):
        v = per * (self.b // 2) + extra
        assert self.it is None or v > 0
        return v if self.it is None else self.it * per + v

    def seq(self):
        return self.b if self.it is None else self.it * 2 + self.b


class Slot:
    def __init__(self, t, it=None):
        self.t, self.it = t, it

    def once(self, offset):
        if (self.t - offset) % SLOTS:
            return None
        return self.chunk(offset)

    def chunk(self, offset):
        b, s = divmod(self.t - offset, SLOTS)
        if self.it is None and not 0 <= b < B:
            return None
        return Step(b, s, self.it)


def wait(eng, sem, value):
    if isinstance(value, int):
        if value > 0:
            eng.wait_ge(sem, value)
    else:
        eng.wait_ge(sem, value)


def run_slots(eng, slot):
    for t in range(LOOP_FROM):
        slot(Slot(t))
    with eng.Fori(0, LOOPS) as it:
        for t in range(BODY):
            slot(Slot(LOOP_FROM + t, it))
    for t in range(LOOP_FROM + BODY * LOOPS, LAST):
        slot(Slot(t))


def previous_use(slot, position, uses):
    for back in range(slot.t + 1):
        earlier = Slot(slot.t - back, slot.it)
        for use in sorted(uses, key=lambda u: -u[1]):
            st = earlier.once(use[0])
            if st and (back or use[1] < position):
                return st, use
    return None


def postln_layer(nc, x, Wqkv, bqkv, Wout, bout, w_gate_up, w_proj, out):
    ctx = ExitStack()
    with ctx:
        def sb(name, shape, dt=F32):
            return ctx.enter_context(nc.sbuf_tensor(name, shape, dt))

        def ps(name, shape, dt=F32):
            return ctx.enter_context(nc.psum_tensor(name, shape, dt))

        def sem(name):
            return ctx.enter_context(nc.semaphore(name))

        NGU = 2 * F // P
        wgu_raw = sb("wgu_raw", [P, NGU, D])
        wp_raw = sb("wp_raw", [P, DT, F])
        NG = (NGU * D + DT * F) // Q_GROUP
        CG = F // Q_GROUP
        w_bf = sb("w_bf", [P, 2, CG, Q_GROUP], BF16)
        w_abs = sb("w_abs", [P, 2, CG, Q_GROUP], BF16)
        w_sign = sb("w_sign", [P, 2, CG, Q_GROUP], BF16)
        w_hat = sb("w_hat", [P, NG, Q_GROUP], BF16)
        w_sum = sb("w_sum", [P, NG])
        w_scale = sb("w_scale", [P, NG], BF16)
        w_half = sb("w_half", [P, NG], BF16)
        wguT = sb("wguT", [P, DT, 2 * F], F32R)
        wpT = sb("wpT", [P, FT, D], F32R)
        wqkv = sb("wqkv", [P, DT, D + 2 * KV])
        wqkv_p = [sb(f"wqkv_{n}", [P, DT, D + 2 * KV], F32R) for n in ("hi", "lo")]
        wo = sb("wo", [P, DT, D])
        wo_p = [sb(f"wo_{n}", [P, DT, D], F32R) for n in ("hi", "lo")]
        bq = sb("bq", [P, DT])
        bq_s = sb("bq_s", [P, DT])
        bk = sb("bk", [KV, 1])
        bv = sb("bv", [P, KV])
        bo = sb("bo", [P, D])
        ident = sb("ident", [P, P])
        ident_bf = sb("ident_bf", [P, P], BF16)
        ones = sb("ones", [P, 1])
        minus_half = sb("minus_half", [P, TT])
        ln_eps = sb("ln_eps", [P, TT])

        xn = sb("xn", [P, 2, TT, D])
        xT = [sb(f"xT_{n}", [P, DT, S], F32R) for n in ("hi", "lo")]
        q_f = sb("q_f", [P, DT, S])
        q_p = sb("q_p", [P, 2, DT, S], F32R)
        k_f = sb("k_f", [KV, S])
        k_p = sb("k_p", [KV, 2, S], F32R)
        q_dram = nc.dram_tensor("q_dram", [2, 2, D, S], F32)
        k_dram = nc.dram_tensor("k_dram", [2, 2, KV, S], F32)
        SROWS = 4 * HD
        XROWS = SROWS + 2
        q_st = sb("q_st", [XROWS, 2, H, S], F32R)
        k_st = sb("k_st", [XROWS, 2, G, S], F32R)
        v_ones = sb("v_ones", [P, 2, TT, G, 2 * HD])
        row_max = sb("row_max", [P, 2, H * TT])
        shift_p = [[sb(f"shift{h}_{n}", [H * TT // 2, P], F32R) for n in ("hi", "lo")] for h in range(2)]
        probs = sb("probs", [P, 2, TT, 2, S])
        pv_sb = sb("pv_sb", [P, 2, S])
        den_r = sb("den_r", [P, 2 * TT * 4])
        att = sb("att", [P, TT, D])
        attT = [sb(f"attT_{n}", [P, DT, S], F32R) for n in ("hi", "lo")]
        res = sb("res", [P, 2, TT, D])
        r1 = sb("r1", [P, TT, D])
        st1 = sb("st1", [P, TT, 6])
        mv1 = sb("mv1", [P, TT, 2])
        ve1 = sb("ve1", [P, TT])
        rstd1 = sb("rstd1", [P, TT])
        x1 = sb("x1", [P, 2, TT, D])
        x1T = [sb(f"x1T_{n}", [P, 2, DT, S], F32R) for n in ("hi", "lo")]
        tanh = sb("tanh", [P, 2, S])
        gated = sb("gated", [P, 2, S])
        h_f = sb("h_f", [P, 2, S])
        h_p = [sb(f"h_{n}", [P, 2, S], F32R) for n in ("hi", "lo")]
        h_sq = sb("h_sq", [P, 2, S])
        sq_sum = sb("sq_sum", [P, 2, S])
        y_sb = sb("y_sb", [P, TT, D])
        ms = sb("ms", [P, TT])
        inv = sb("inv", [P, TT])
        r2 = sb("r2", [P, TT, D])
        st2 = sb("st2", [P, TT, 6])
        mv2 = sb("mv2", [P, TT, 2])
        ve2 = sb("ve2", [P, TT])
        rstd2 = sb("rstd2", [P, TT])
        y_out = sb("y_out", [P, 2, TT, D])

        max_ps = ps("max_ps", [P, 2 * TT, S])
        exp_ps = ps("exp_ps", [P, TT, 2 * S])
        ffn_ps = ps("ffn_ps", [P, 2, S])
        down_ps = ps("down_ps", [P, TT, D])
        pv_ps = ps("pv_ps", [P, 2, S])
        misc_ps = ps("misc_ps", [P, 512])

        w_loaded = [sem(f"w_loaded{i}") for i in range(3)]
        consts_made, k_ones = sem("consts_made"), sem("k_ones")
        w_act, w_red, w_dve, w_tr, w_ev = sem("w_act"), sem("w_red"), sem("w_dve"), sem("w_tr"), sem("w_ev")
        w_split_hi, w_split = sem("w_split_hi"), sem("w_split")
        x_loaded = [sem(f"x_loaded{i}") for i in range(2)]
        res_loaded = [sem(f"res_loaded{i}") for i in range(2)]
        xT_made, xT_hi, xT_lo = sem("xT_made"), sem("xT_hi"), sem("xT_lo")
        q_made, q_copied, q_lo = sem("q_made"), sem("q_copied"), sem("q_lo")
        k_made, k_copied, k_lo = sem("k_made"), sem("k_copied"), sem("k_lo")
        v_made, v_copied = sem("v_made"), sem("v_copied")
        qk_saved = [sem(f"qk_saved{i}") for i in range(2)]
        qk_stacked = [sem(f"qk_stacked{i}") for i in range(2)]
        max_scored, max_taken = sem("max_scored"), sem("max_taken")
        shift_turned, shift_split = sem("shift_turned"), sem("shift_split")
        shift_hi = sem("shift_hi")
        shift_loaded = [sem(f"shift_loaded{i}") for i in range(2)]
        exp_scored, exp_done = sem("exp_scored"), sem("exp_done")
        pv_done, pv_copied, pv_turned = sem("pv_done"), sem("pv_copied"), sem("pv_turned")
        den_done, att_done = sem("den_done"), sem("att_done")
        att_turned, attT_hi, attT_lo = sem("att_turned"), sem("attT_hi"), sem("attT_lo")
        bout_added, o_made = sem("bout_added"), sem("o_made")
        r1_done, bn1_done, var1_done, ve1_done, rstd1_done, x1_done = (
            sem("r1_done"), sem("bn1_done"), sem("var1_done"), sem("ve1_done"), sem("rstd1_done"), sem("x1_done"))
        x1_turned, x1T_hi, x1T_lo = sem("x1_turned"), sem("x1T_hi"), sem("x1T_lo")
        ffn_made, tanh_done, gated_done, h_done = sem("ffn_made"), sem("tanh_done"), sem("gated_done"), sem("h_done")
        h_hi, h_squared, h_lo, h_summed = sem("h_hi"), sem("h_squared"), sem("h_lo"), sem("h_summed")
        down_done, y_copied, sq_summed, ms_done, inv_done = (
            sem("down_done"), sem("y_copied"), sem("sq_summed"), sem("ms_done"), sem("inv_done"))
        r2_done, bn2_done, var2_done, ve2_done, rstd2_done, y_done = (
            sem("r2_done"), sem("bn2_done"), sem("var2_done"), sem("ve2_done"), sem("rstd2_done"), sem("y_done"))
        waited, sp_waited = sem("waited"), sem("sp_waited")
        stored = [sem(f"stored{i}") for i in range(2)]

        GPT = D // Q_GROUP
        chunks = [(wgu_raw[:, 4 * c:4 * c + 4, :], 4 * c * GPT, 4 * GPT) for c in range(NGU // 4)]
        chunks += [(wp_raw[:, c:c + 1, :], (NGU * D + c * F) // Q_GROUP, F // Q_GROUP) for c in range(DT)]
        NCH = len(chunks)

        turns = []
        for r in range(NGU):
            if r % 2 == 0:
                turns.append((r // 4, [(w_hat, ((r + a) * D + k * P), ("gu", k, (r + a) * P)) for k in range(DT) for a in range(2)],
                              wguT[:, :, r * P:(r + 2) * P]))
        for k in range(0, FT, 2):
            turns.append((NCH - 1, [(w_hat, NGU * D + r * F + (k + a) * P, None) for a in range(2) for r in range(DT)],
                          wpT[:, k:k + 2, :]))

        block = ctx.enter_context(nc.Block())

        @block.sync
        def _(sp):
            sp.dma_start(xn[:, 0], x[0].rearrange("(t p) d -> p t d", p=P)).then_inc(x_loaded[0], 16)
            sp.dma_start(wqkv[:], Wqkv.rearrange("(t p) n -> p t n", p=P)).then_inc(w_loaded[0], 16)
            for g in range(G):
                for i in range(2):
                    at, row = 64 * (g // 2) + HD * quadrant(g, i), HD * (g + 4 * i)
                    sp.dma_start(wo[at:at + HD], Wout.rearrange("(h r) n -> r h n", h=2)[row:row + HD]
                                 ).then_inc(w_loaded[0], 16)
            with nc.allow_non_contiguous_dma("bias columns"):
                sp.dma_start(bq[:], bqkv[0:D].rearrange("(t p) -> p t", p=P)).then_inc(w_loaded[0], 16)
                sp.dma_start(bk[:], bqkv[D:D + KV].rearrange("(p o) -> p o", o=1)).then_inc(w_loaded[0], 16)
            sp.dma_start(bv[:], bqkv[D + KV:D + 2 * KV].partition_broadcast(P)).then_inc(w_loaded[0], 16)
            sp.dma_start(bo[:], bout.partition_broadcast(P)).then_inc(w_loaded[0], 16)
            sp.dma_start(wgu_raw[:], w_gate_up.rearrange("(t p) d -> p t d", p=P)).then_inc(w_loaded[1], 16)
            sp.dma_start(wp_raw[:], w_proj.rearrange("(t p) d -> p t d", p=P)).then_inc(w_loaded[2], 16)

            def sp_wait(semaphore, value):
                wait(sp, semaphore, value)
                if not isinstance(value, int):
                    sp.sem_inc(sp_waited, 1)

            def slot(n):
                for half in range(2):
                    if st := n.once(SHIFT_T[half]):
                        sp_wait(shift_split, st.count(2, half + 1))
                        for part in range(2):
                            sp.dma_start(
                                q_st[SROWS + part:SROWS + part + 1, st.par, half * H // 2:(half + 1) * H // 2, :]
                                .bitcast(F32), shift_p[half][part][:].bitcast(F32)).then_inc(shift_loaded[half], 16)
                if st := n.once(SAVE_QK):
                    sp_wait(q_lo, st.count(1, 1))
                    sp_wait(k_lo, st.count(1, 1))
                    sp_wait(qk_stacked[st.par], st.count2(128, 0))
                    sp.dma_start(q_dram[st.par].rearrange("a (m p) t -> p a m t", p=P), q_p[:].bitcast(F32)
                                 ).then_inc(qk_saved[st.par], 16)
                    sp.dma_start(k_dram[st.par].rearrange("a p t -> p a t"), k_p[:].bitcast(F32)
                                 ).then_inc(qk_saved[st.par], 16)
                if st := n.once(STACK_QK):
                    sp_wait(qk_saved[st.par], st.count2(32, 32))
                    sp_wait(exp_scored, st.count(8, -8))
                    for c in range(4):
                        sp.dma_start(
                            k_st[c * HD:(c + 1) * HD, st.par].bitcast(F32),
                            k_dram[st.par, c % 2].rearrange("(g d) t -> d g t", d=HD)).then_inc(qk_stacked[st.par], 16)
                        sp.dma_start(
                            q_st[c * HD:(c + 1) * HD, st.par].bitcast(F32),
                            q_dram[st.par, c // 2].rearrange("(h d) t -> d h t", d=HD)
                        ).then_inc(qk_stacked[st.par], 16)
                if (st := n.once(LOAD_X)) and not (st.it is None and st.b == 0):
                    sp_wait(xT_made, st.count(1, -1))
                    sp.dma_start(xn[:, st.par], x[st.seq()].rearrange("(t p) d -> p t d", p=P)
                                 ).then_inc(x_loaded[st.par], 16)
                if st := n.once(LOAD_RES):
                    sp_wait(r1_done, st.count(1, -1))
                    sp.dma_start(res[:, st.par], x[st.seq()].rearrange("(t p) d -> p t d", p=P)
                                 ).then_inc(res_loaded[st.par], 16)
                if st := n.once(STORE):
                    sp_wait(y_done, st.count(TT, TT))
                    sp.dma_start(out[st.seq()].rearrange("(t p) d -> p t d", p=P), y_out[:, st.par]
                                 ).then_inc(stored[st.par], 16)

            run_slots(sp, slot)
            for i in range(2):
                sp.wait_ge(stored[i], 16 * B // 2)

        @block.tensor
        def _(pe):
            def products(dst, lhs, rhs, start=True, stop=True):
                pairs = list(zip(lhs, rhs))
                for i, (a, b) in enumerate(pairs):
                    last = pe.matmul(dst, a, b, start=start and i == 0, stop=stop and i == len(pairs) - 1)
                return last

            pe.wait_ge(consts_made, 3)
            for n, (chunk, blocks, _) in enumerate(turns):
                pe.wait_ge(w_dve, 5 * (chunk + 1))
                if n:
                    pe.wait_ge(w_ev, n)
                for i, (w, at, _) in enumerate(blocks):
                    flat = w[:].rearrange("p g e -> p (g e)")
                    last = pe.transpose(misc_ps[:].bitcast(BF16)[:, i * P:(i + 1) * P], flat[:, at:at + P], ident_bf[:])
                last.then_inc(w_tr, 1)
            pe.wait_ge(w_ev, len(turns))
            pe.wait_ge(w_split, 2)
            pe.wait_ge(k_ones, 1)

            misc_users = [
                (PROJ_V, 0, v_copied, 1, 1), (ATT_T, 1, attT_lo, 1, 1), (X_T, 0, xT_lo, 1, 1), (PROJ_O, 1, r1_done, 1, 1),
                (PROJ_Q, 0, q_copied, 1, 1), (PROJ_K, 1, k_copied, 1, 1), (SHIFT_T[0], 0, shift_split, 2, 1),
                (X1_T, 1, x1T_lo, 1, 1), (PV_T[0], 0, att_done, 4, 2), (SUM_SQ, 0, ms_done, 1, 1),
                (PV_T[1], 0, att_done, 4, 4), (SHIFT_T[1], 0, shift_split, 2, 2)]

            def use_misc(n, pos):
                if found := previous_use(n, pos, misc_users):
                    st, (_, _, released, per, extra) = found
                    wait(pe, released, st.count(per, extra))

            def max_scores(st):
                wait(pe, qk_stacked[st.par], st.count2(128, 128))
                wait(pe, max_taken, st.count(8, st.s))
                for i in range(2):
                    head = first_head(st.s) + 4 * i
                    for t in range(TT):
                        last = pe.matmul(max_ps[:, 2 * i + t, :], q_st[0:SROWS, st.par, head, t * P:(t + 1) * P],
                                         k_st[0:SROWS, st.par, st.s % 4, :], start=True, stop=True)
                last.then_inc(max_scored, 1)

            def exp_scores(st):
                wait(pe, shift_loaded[st.s // 4], st.count(32, 32))
                wait(pe, exp_done, st.count(8, st.s))
                for t in range(TT):
                    last = pe.matmul(exp_ps[:, t, :], k_st[:, st.par, st.s % 4, t * P:(t + 1) * P],
                                     q_st[:, st.par, first_head(st.s):first_head(st.s) + 5:4, :], start=True, stop=True)
                last.then_inc(exp_scored, 1)

            def gate_up(st):
                wait(pe, x1T_lo, st.count(1, 1))
                wait(pe, h_done, st.count(8, st.s))
                for half in range(2):
                    c = half * F + st.s * P
                    last = products(ffn_ps[:, half, :],
                                    [wguT[:, k, c:c + P] for k in range(DT) for _ in range(2)],
                                    [x1T[a][:, st.par, k, :] for k in range(DT) for a in range(2)])
                last.then_inc(ffn_made, 1)

            def down(st):
                wait(pe, h_lo, st.count(8, st.s + 1))
                wait(pe, h_hi, st.count(8, st.s + 1))
                if st.s == 0:
                    wait(pe, y_copied, st.count(1, 0))
                for t in range(TT):
                    for a in range(2):
                        last = pe.matmul(down_ps[:, t, :], h_p[a][:, st.s % 2, t * P:(t + 1) * P], wpT[:, st.s, :],
                                         start=(st.s == 0 and t == 0 and a == 0), stop=(st.s == FT - 1 and a == 1),
                                         skip_group_check=True)
                last.then_inc(down_done, 1)

            def times_v(st):
                wait(pe, exp_done, st.count(8, st.s + 1))
                wait(pe, v_copied, st.count(1, 1))
                if st.s % 4 == 0:
                    wait(pe, pv_copied, st.count(2, st.s // 4))
                g = st.s % 4
                for t in range(TT):
                    for i in range(2):
                        r = 32 * quadrant(g, i)
                        last = pe.matmul(pv_ps[r:r + 32, g // 2, :], v_ones[:, st.par, t, g, :],
                                         probs[:, st.s % 2, t, i, :], start=(t == 0), stop=(t == TT - 1),
                                         tile_position=(0, r))
                last.then_inc(pv_done, 1)

            def turn(src, done):
                for i, blk in enumerate(src):
                    last = pe.transpose(misc_ps[:, i * P:(i + 1) * P], blk, ident[:])
                last.then_inc(done, 1)

            def slot(n):
                if st := n.chunk(MAX0):
                    max_scores(st)
                if st := n.chunk(EXP0):
                    exp_scores(st)
                if st := n.chunk(FFN0):
                    gate_up(st)
                if st := n.once(PROJ_V):
                    use_misc(n, 0)
                    wait(pe, xT_lo, st.count(1, 1))
                    for t in range(TT):
                        last = products(misc_ps[:, t * KV:(t + 1) * KV],
                                        [xT[a][:, k, t * P:(t + 1) * P] for k in range(DT) for a in range(2) for _ in range(2)],
                                        [wqkv_p[c][:, k, D + KV:D + 2 * KV] for k in range(DT) for _ in range(2) for c in range(2)])
                    last.then_inc(v_made, 1)
                if st := n.once(X_T):
                    use_misc(n, 0)
                    wait(pe, x_loaded[st.par], st.count2(16, 16))
                    turn([xn[:, st.par, t, k * P:(k + 1) * P] for k in range(DT) for t in range(TT)], xT_made)
                if st := n.once(PROJ_Q):
                    use_misc(n, 0)
                    wait(pe, xT_lo, st.count(1, 1))
                    for m in range(DT):
                        last = products(misc_ps[:, m * S:(m + 1) * S],
                                        [wqkv_p[c][:, k, m * P:(m + 1) * P] for k in range(DT) for c in range(2) for _ in range(2)],
                                        [xT[a][:, k, :] for k in range(DT) for _ in range(2) for a in range(2)])
                    last.then_inc(q_made, 1)
                for half in range(2):
                    if st := n.once(SHIFT_T[half]):
                        use_misc(n, 0)
                        wait(pe, max_taken, st.count(8, 4 * half + 4))
                        pe.transpose(misc_ps[0:H * TT // 2, 0:P], row_max[:, st.par, half * H:(half + 1) * H], ident[:]
                                     ).then_inc(shift_turned, 1)
                    if st := n.once(PV_T[half]):
                        use_misc(n, 0)
                        wait(pe, pv_copied, st.count(2, half + 1))
                        turn([pv_sb[:, g, t * P:(t + 1) * P] for g in range(2) for t in range(TT)], pv_turned)
                if st := n.once(SUM_SQ):
                    use_misc(n, 0)
                    wait(pe, h_summed, st.count(FT - 1, FT - 1))
                    for t in range(TT):
                        last = pe.matmul(misc_ps[:, t:t + 1], sq_sum[:, st.par, t * P:(t + 1) * P], ones[:],
                                         start=True, stop=True)
                    last.then_inc(sq_summed, 1)
                if st := n.chunk(PV0):
                    times_v(st)
                if st := n.once(ATT_T):
                    use_misc(n, 1)
                    wait(pe, att_done, st.count(4, 4))
                    turn([att[:, t, m * P:(m + 1) * P] for m in range(DT) for t in range(TT)], att_turned)
                if st := n.once(PROJ_O):
                    use_misc(n, 1)
                    wait(pe, attT_lo, st.count(1, 1))
                    for t in range(TT):
                        last = products(misc_ps[:, t * D:(t + 1) * D],
                                        [attT[a][:, m, t * P:(t + 1) * P] for m in range(DT) for a in range(2) for _ in range(2)],
                                        [wo_p[c][:, m, :] for m in range(DT) for _ in range(2) for c in range(2)])
                    last.then_inc(o_made, 1)
                if st := n.once(PROJ_K):
                    use_misc(n, 1)
                    last = products(misc_ps[0:KV, 0:S],
                                    [wqkv_p[c][:, k, D:D + KV] for k in range(DT) for c in range(2) for _ in range(2)],
                                    [xT[a][:, k, :] for k in range(DT) for _ in range(2) for a in range(2)])
                    last.then_inc(k_made, 1)
                if st := n.once(X1_T):
                    use_misc(n, 1)
                    wait(pe, x1_done, st.count(TT, TT))
                    turn([x1[:, st.par, t, k * P:(k + 1) * P] for k in range(DT) for t in range(TT)], x1_turned)
                if st := n.chunk(DOWN0):
                    down(st)

            run_slots(pe, slot)

        @block.scalar
        def _(act):
            for c, (raw, g0, ng) in enumerate(chunks):
                act.wait_ge(w_loaded[1 if c < NCH - DT else 2], 16)
                if c >= 2:
                    act.wait_ge(w_dve, 5 * (c - 1))
                flat = w_bf[:, c % 2].rearrange("p g e -> p (g e)")
                act.activation(flat, raw.rearrange("p a b -> p (a b)"), ACT.Identity).then_inc(w_act, 1)
                act.wait_ge(w_act, 3 * c + 1)
                act.activation(w_abs[:, c % 2].rearrange("p g e -> p (g e)"), flat, ACT.Abs).then_inc(w_act, 1)
                act.activation(w_sign[:, c % 2].rearrange("p g e -> p (g e)"), flat, ACT.Sign).then_inc(w_act, 1)
            act.wait_ge(w_loaded[0], 16 * 13)
            act.activation(wqkv_p[0][:], wqkv[:], ACT.Identity).then_inc(w_split_hi, 1)
            act.activation(wo_p[0][:], wo[:], ACT.Identity).then_inc(w_split_hi, 1)
            act.activation(bq_s[:], bq[:], ACT.Identity, scale=1.0 / HD).then_inc(w_split_hi, 1)
            act.wait_ge(w_split_hi, 3)

            def high(dst, src):
                return act.activation(dst, src, ACT.Identity)

            def slot(n):
                if st := n.chunk(EXP0):
                    wait(act, exp_scored, st.count(8, st.s + 1))
                    wait(act, pv_done, st.count(8, st.s - 1))
                    act.activation(probs[:, st.s % 2], exp_ps[:], ACT.Exp).then_inc(exp_done, 1)
                if st := n.chunk(FFN0):
                    wait(act, ffn_made, st.count(8, st.s + 1))
                    wait(act, gated_done, st.count(8, st.s - 1))
                    act.activation(tanh[:, st.s % 2, :], ffn_ps[:, 0, :], ACT.Tanh, scale=0.5).then_inc(tanh_done, 1)
                if st := n.once(X_T):
                    wait(act, xT_made, st.count(1, 1))
                    wait(act, v_made, st.count(1, 0))
                    high(xT[0][:], misc_ps[:].rearrange("p (k t) -> p k t", k=DT)).then_inc(xT_hi, 1)
                if st := n.once(PROJ_Q):
                    wait(act, q_made, st.count(1, 1))
                    wait(act, q_lo, st.count(1, 0))
                    if st.it is not None or st.b > 0:
                        wait(act, qk_saved[1 - st.par], Step(st.b - 1, 0, st.it).count2(32, 32))
                    for m in range(DT):
                        for dst in (q_f[:, m, :], q_p[:, 0, m, :]):
                            last = act.activation(dst, misc_ps[:, m * S:(m + 1) * S], ACT.Identity,
                                                  bias=bq_s[:, m:m + 1], scale=1.0 / HD)
                    last.then_inc(q_copied, 1)
                if st := n.once(X1_T):
                    wait(act, x1_turned, st.count(1, 1))
                    wait(act, ffn_made, st.count(8, -8))
                    high(x1T[0][:, st.par], misc_ps[:].rearrange("p (k t) -> p k t", k=DT)).then_inc(x1T_hi, 1)
                if st := n.once(ATT_T):
                    wait(act, att_turned, st.count(1, 1))
                    wait(act, o_made, st.count(1, 0))
                    high(attT[0][:], misc_ps[:].rearrange("p (k t) -> p k t", k=DT)).then_inc(attT_hi, 1)
                if st := n.once(PROJ_K):
                    wait(act, k_made, st.count(1, 1))
                    wait(act, k_lo, st.count(1, 0))
                    for dst in (k_f[:], k_p[:, 0, :]):
                        last = act.activation(dst, misc_ps[0:KV, 0:S], ACT.Identity, bias=bk[:, 0:1])
                    last.then_inc(k_copied, 1)
                if st := n.chunk(FFN0):
                    wait(act, h_done, st.count(8, st.s + 1))
                    wait(act, down_done, st.count(8, st.s - 1))
                    high(h_p[0][:, st.s % 2, :], h_f[:, st.s % 2, :]).then_inc(h_hi, 1)
                    if st.s == 0:
                        wait(act, sq_summed, st.count(1, -1))
                        dst = sq_sum[:, st.par, :]
                    else:
                        wait(act, h_summed, st.count(FT - 1, max(st.s - 2, 0)))
                        dst = h_sq[:, st.s % 2, :]
                    act.activation(dst, h_f[:, st.s % 2, :], ACT.Square).then_inc(h_squared, 1)
                for half in range(2):
                    if st := n.once(PV_COPY[half]):
                        wait(act, pv_done, st.count(8, 4 * half + 4))
                        wait(act, pv_turned, st.count(2, half))
                        act.activation(pv_sb[:], pv_ps[:], ACT.Identity).then_inc(pv_copied, 1)
                if st := n.once(Y_COPY):
                    wait(act, down_done, st.count(8, 8))
                    wait(act, r2_done, st.count(TT, 0))
                    act.activation(y_sb[:], down_ps[:], ACT.Identity).then_inc(y_copied, 1)

            run_slots(act, slot)

        @block.vector
        def _(dve):
            dve.memset(k_st[SROWS:XROWS].bitcast(F32), 1.0).then_inc(k_ones, 1)
            nd = 0
            for c, (_, g0, ng) in enumerate(chunks):
                gs = slice(g0, g0 + ng)
                dve.wait_ge(w_act, 3 * c + 3)
                dve.tensor_reduce(w_sum[:, gs], w_abs[:, c % 2], AX.X, ALU.add).then_inc(w_red, 1)
                dve.wait_ge(w_red, 3 * c + 1)
                dve.tensor_scalar(w_scale[:, gs], w_sum[:, gs], 1.0 / Q_GROUP, 1e-8, ALU.mult, ALU.max).then_inc(w_red, 1)
                dve.wait_ge(w_red, 3 * c + 2)
                dve.tensor_scalar(w_half[:, gs], w_scale[:, gs], 0.5, None, ALU.mult).then_inc(w_red, 1)
                dve.wait_ge(w_red, 3 * c + 3)
                half = w_half[:, gs].unsqueeze(2).broadcast_to([P, ng, Q_GROUP])
                scale = w_scale[:, gs].unsqueeze(2).broadcast_to([P, ng, Q_GROUP])
                hat = w_hat[:, gs, :]
                for a, b, op in ((w_abs[:, c % 2], half, ALU.is_gt), (hat, scale, ALU.mult), (hat, w_sign[:, c % 2], ALU.mult),
                                 (hat, w_bf[:, c % 2], ALU.subtract), (hat, w_bf[:, c % 2], ALU.add)):
                    if nd:
                        dve.wait_ge(w_dve, nd)
                    dve.tensor_tensor(hat, a, b, op).then_inc(w_dve, 1)
                    nd += 1
            for n, (_, blocks, dst) in enumerate(turns):
                dve.wait_ge(w_tr, n + 1)
                dve.tensor_copy(dst, misc_ps[:].bitcast(BF16)[:, 0:4 * P].rearrange("p (k t) -> p k t", k=2)
                                ).then_inc(w_ev, 1)
            dve.wait_ge(w_split_hi, 2)
            dve.tensor_tensor(wqkv_p[1][:], wqkv[:], wqkv_p[0][:].bitcast(F32), ALU.subtract).then_inc(w_split, 1)
            dve.tensor_tensor(wo_p[1][:], wo[:], wo_p[0][:].bitcast(F32), ALU.subtract).then_inc(w_split, 1)

            def low(dst, src, hi):
                return dve.tensor_tensor(dst, src, hi.bitcast(F32), ALU.subtract)

            def misc2():
                return misc_ps[:].rearrange("p (k t) -> p k t", k=2)

            def slot(n):
                if st := n.once(LN2_STATS):
                    wait(dve, inv_done, st.count(1, 1))
                    wait(dve, y_copied, st.count(1, 1))
                    for t in range(TT):
                        dve.scalar_tensor_tensor(r2[:, t, :], y_sb[:, t, :], inv[:, t:t + 1], x1[:, st.par, t, :],
                                                 ALU.mult, ALU.add).then_inc(r2_done, 1)
                    for t in range(TT):
                        wait(dve, r2_done, st.count(TT, t + 1))
                        dve.bn_stats(st2[:, t, :], r2[:, t, :]).then_inc(bn2_done, 1)
                    wait(dve, bn2_done, st.count(TT, TT))
                    dve.sem_inc(waited, 1)
                    for t in range(TT):
                        dve.bn_aggr(mv2[:, t, :], st2[:, t, :]).then_inc(var2_done, 1)
                if st := n.once(LN2_APPLY):
                    wait(dve, rstd2_done, st.count(1, 1))
                    wait(dve, stored[st.par], st.count2(16, 0))
                    for t in range(TT):
                        dve.tensor_scalar(y_out[:, st.par, t, :], r2[:, t, :], mv2[:, t, 0:1], rstd2[:, t:t + 1],
                                          ALU.subtract, ALU.mult).then_inc(y_done, 1)
                if st := n.once(LN1_APPLY):
                    wait(dve, rstd1_done, st.count(1, 1))
                    for t in range(TT):
                        dve.tensor_scalar(x1[:, st.par, t, :], r1[:, t, :], mv1[:, t, 0:1], rstd1[:, t:t + 1],
                                          ALU.subtract, ALU.mult).then_inc(x1_done, 1)
                if st := n.chunk(MAX0):
                    wait(dve, max_scored, st.count(8, st.s + 1))
                    if st.s == 0:
                        wait(dve, shift_turned, st.count(2, -2))
                    head = first_head(st.s)
                    dve.tensor_reduce(row_max[:, st.par].rearrange("p (h t) -> p h t", t=TT)[:, head:head + 5:4, :],
                                      max_ps[:].rearrange("p (i t) k -> p i t k", i=2), AX.X, ALU.max
                                      ).then_inc(max_taken, 1)
                if st := n.chunk(FFN0):
                    wait(dve, tanh_done, st.count(8, st.s + 1))
                    dve.scalar_tensor_tensor(gated[:, st.s % 2, :], tanh[:, st.s % 2, :], 1.0, ffn_ps[:, 0, :],
                                             ALU.add, ALU.mult).then_inc(gated_done, 1)
                    wait(dve, gated_done, st.count(8, st.s + 1))
                    wait(dve, h_lo, st.count(8, st.s - 1))
                    wait(dve, h_squared, st.count(8, st.s - 1))
                    dve.tensor_tensor(h_f[:, st.s % 2, :], gated[:, st.s % 2, :], ffn_ps[:, 1, :], ALU.mult
                                      ).then_inc(h_done, 1)
                if st := n.once(PROJ_V):
                    wait(dve, v_made, st.count(1, 1))
                    wait(dve, pv_done, st.count(8, -8))
                    for t in range(TT):
                        last = dve.tensor_tensor(
                            v_ones[:, st.par, t, :, 0:HD],
                            misc_ps[:, t * KV:(t + 1) * KV].rearrange("p (g d) -> p g d", g=G),
                            bv[:].rearrange("p (g d) -> p g d", g=G), ALU.add)
                    last.then_inc(v_copied, 1)
                if st := n.once(X_T):
                    wait(dve, xT_hi, st.count(1, 1))
                    low(xT[1][:], misc2(), xT[0][:]).then_inc(xT_lo, 1)
                if st := n.once(PROJ_K):
                    wait(dve, k_copied, st.count(1, 1))
                    low(k_p[:, 1, :], k_f[:], k_p[:, 0, :]).then_inc(k_lo, 1)
                for half in range(2):
                    if st := n.once(SHIFT_T[half]):
                        src = misc_ps[0:H * TT // 2, 0:P]
                        hi, lo = shift_p[half]
                        wait(dve, shift_turned, st.count(2, half + 1))
                        wait(dve, shift_loaded[half], st.count(32, 0))
                        dve.tensor_scalar(hi[:], src, -1.0, None, ALU.mult).then_inc(shift_hi, 1)
                        wait(dve, shift_hi, st.count(2, half + 1))
                        dve.scalar_tensor_tensor(lo[:], src, -1.0, hi[:].bitcast(F32), ALU.mult, ALU.subtract
                                                 ).then_inc(shift_split, 1)
                    if st := n.once(PV_T[half]):
                        pv = misc_ps[:].rearrange("p (g t j e) -> p g t j e", g=2, t=TT, j=4)
                        rec = den_r[:].rearrange("p (g t j) -> p g t j", g=2, t=TT)
                        wait(dve, pv_turned, st.count(2, half + 1))
                        wait(dve, att_done, st.count(4, 2 * half))
                        dve.reciprocal(rec.rearrange("p g t j -> p (g t) j"),
                                       pv.rearrange("p g t j e -> p (g t) j e")[:, :, :, HD]).then_inc(den_done, 1)
                        wait(dve, den_done, st.count(2, half + 1))
                        if half == 0:
                            wait(dve, att_turned, st.count(1, 0))
                        for i in range(2):
                            last = dve.tensor_tensor(
                                att[:].rearrange("p t (h i j d) -> p t h i j d", h=2, i=2, j=4)[:, :, half, i],
                                pv[:, i, :, :, 0:HD],
                                rec[:, i].unsqueeze(3).broadcast_to([P, TT, 4, HD]), ALU.mult).then_inc(att_done, 1)
                        last
                if st := n.once(SUM_SQ):
                    wait(dve, sq_summed, st.count(1, 1))
                    dve.tensor_scalar(ms[:], misc_ps[:, 0:TT], 1.0 / F, 4.0 * RMS_EPS, ALU.mult, ALU.add
                                      ).then_inc(ms_done, 1)
                if st := n.once(ATT_T):
                    wait(dve, attT_hi, st.count(1, 1))
                    low(attT[1][:], misc2(), attT[0][:]).then_inc(attT_lo, 1)
                if st := n.once(PROJ_O):
                    wait(dve, o_made, st.count(1, 1))
                    wait(dve, bout_added, st.count(1, 1))
                    dve.tensor_tensor(r1[:], misc2(), res[:, st.par], ALU.add).then_inc(r1_done, 1)
                    wait(dve, r1_done, st.count(1, 1))
                    for t in range(TT):
                        dve.bn_stats(st1[:, t, :], r1[:, t, :]).then_inc(bn1_done, 1)
                    wait(dve, bn1_done, st.count(TT, TT))
                    dve.sem_inc(waited, 1)
                    for t in range(TT):
                        dve.bn_aggr(mv1[:, t, :], st1[:, t, :]).then_inc(var1_done, 1)
                if st := n.once(X1_T):
                    wait(dve, x1T_hi, st.count(1, 1))
                    low(x1T[1][:, st.par], misc2(), x1T[0][:, st.par]).then_inc(x1T_lo, 1)

            run_slots(dve, slot)

        @block.gpsimd
        def _(pool):
            pool.memset(ident[:], 0.0).then_inc(consts_made, 1)
            pool.memset(ones[:], 1.0)
            pool.memset(minus_half[:], -0.5)
            pool.memset(ln_eps[:], LN_EPS)
            pool.memset(v_ones[:], 1.0)
            pool.wait_ge(consts_made, 1)
            pool.affine_select(out=ident[:], in_=ident[:], compare_op=ALU.not_equal, fill=1.0, base=0,
                               pattern=[[-1, P]], channel_multiplier=1).then_inc(consts_made, 1)
            pool.wait_ge(consts_made, 2)
            pool.tensor_copy(ident_bf[:], ident[:]).then_inc(consts_made, 1)

            def rsqrt(dst, src, done):
                pool.tensor_tensor(dst, src, minus_half[:], ALU.pow).then_inc(done, 1)

            def slot(n):
                if st := n.chunk(FFN0):
                    wait(pool, h_hi, st.count(8, st.s + 1))
                    wait(pool, down_done, st.count(8, st.s - 1))
                    pool.tensor_tensor(h_p[1][:, st.s % 2, :], h_f[:, st.s % 2, :],
                                       h_p[0][:, st.s % 2, :].bitcast(F32), ALU.subtract).then_inc(h_lo, 1)
                    if st.s:
                        wait(pool, h_squared, st.count(8, st.s + 1))
                        wait(pool, h_summed, st.count(FT - 1, st.s - 1))
                        pool.tensor_tensor(sq_sum[:, st.par, :], sq_sum[:, st.par, :], h_sq[:, st.s % 2, :], ALU.add
                                           ).then_inc(h_summed, 1)
                if st := n.once(PROJ_Q):
                    wait(pool, q_copied, st.count(1, 1))
                    pool.tensor_tensor(q_p[:, 1], q_f[:], q_p[:, 0].bitcast(F32), ALU.subtract).then_inc(q_lo, 1)
                if st := n.once(ADD_BOUT):
                    wait(pool, res_loaded[st.par], st.count2(16, 16))
                    for t in range(TT):
                        last = pool.tensor_tensor(res[:, st.par, t, :], res[:, st.par, t, :], bo[:], ALU.add)
                    last.then_inc(bout_added, 1)
                if st := n.once(PROJ_O):
                    wait(pool, var1_done, st.count(TT, TT))
                    pool.tensor_tensor(ve1[:], mv1[:, :, 1], ln_eps[:], ALU.add).then_inc(ve1_done, 1)
                    wait(pool, ve1_done, st.count(1, 1))
                    rsqrt(rstd1[:], ve1[:], rstd1_done)
                if st := n.once(SUM_SQ):
                    wait(pool, ms_done, st.count(1, 1))
                    rsqrt(inv[:], ms[:], inv_done)
                if st := n.once(LN2_STATS):
                    wait(pool, var2_done, st.count(TT, TT))
                    pool.tensor_tensor(ve2[:], mv2[:, :, 1], ln_eps[:], ALU.add).then_inc(ve2_done, 1)
                    wait(pool, ve2_done, st.count(1, 1))
                    rsqrt(rstd2[:], ve2[:], rstd2_done)

            run_slots(pool, slot)


_INS = ["L0_attn_x", "L0_attn_Wqkv", "L0_attn_bqkv", "L0_attn_Wout", "L0_attn_bout", "L0_ffn_w_gate_up",
        "L0_ffn_w_proj"]


def kernel(**inputs):
    import numpy as _np
    import concourse.bacc as _bacc
    from concourse import mybir as _mybir
    from concourse.bass_utils import run_bass_kernel_spmd as _run

    nc = _bacc.Bacc("TRN2", target_bir_lowering=False, num_devices=1)
    arrays, args = {}, []
    for name in _INS:
        a = _np.ascontiguousarray(inputs[name])
        arrays[f"in_{name}_dram"] = a
        args.append(nc.dram_tensor(f"in_{name}_dram", a.shape, _mybir.dt.from_np(a.dtype), kind="ExternalInput").ap())
    out = nc.dram_tensor("out_0_dram", (B, S, D), _mybir.dt.float32, kind="ExternalOutput").ap()
    postln_layer(nc, *args, out)
    r = _run(nc, [arrays], core_ids=[0])
    return r.results[0]["out_0_dram"]
```

```python
from contextlib import ExitStack

import concourse.bass as bass
from concourse import mybir

ALU = mybir.AluOpType
ACT = mybir.ActivationFunctionType
AX = mybir.AxisListType
F32 = mybir.dt.float32
F32R = mybir.dt.float32r
BF16 = mybir.dt.bfloat16

P = 128
B, S, D = 16, 256, 256
H, G, HD = 16, 4, 16
KV = G * HD
F = 4 * D
TT = S // P
DT = D // P
FT = F // P
Q_GROUP = 64
LN_EPS = 1e-5
RMS_EPS = 2.0 ** -23

SLOTS = 8
LOAD_X, X_T, PROJ_Q, PROJ_K, SAVE_QK, STACK_QK, MAX0, PROJ_V = 0, 1, 2, 2, 3, 4, 6, 8
SHIFT_T = (11, 15)
EXP0 = 13
PV0 = EXP0 + 1
PV_COPY = (PV0 + 3, PV0 + 7)
PV_T = (20, 22)
LOAD_RES, ADD_BOUT, ATT_T, PROJ_O, LN1_APPLY, X1_T = 23, 24, 24, 25, 26, 27
FFN0 = 28
DOWN0 = FFN0 + 1
SUM_SQ, LN2_STATS, LN2_APPLY = 37, 38, 39
Y_COPY = DOWN0 + 7
STORE = 39
READ_W0, TURN_W0, WO_SPLIT = 1, 2, 14

LAST = SLOTS * B + STORE
LOOP_FROM, BODY = 48, 2 * SLOTS
LOOPS = (SLOTS * B - LOOP_FROM) // BODY


def first_head(c):
    return 8 * (c // 4) + c % 4


def quadrant(g, i):
    return 2 * (g % 2) + i


class Step:

    def __init__(self, b, s, it):
        self.b, self.s, self.it = b, s, it
        self.par = b % 2

    def count(self, per, extra):
        v = per * self.b + extra
        assert self.it is None or v > 0
        return v if self.it is None else self.it * (2 * per) + v

    def count2(self, per, extra):
        v = per * (self.b // 2) + extra
        assert self.it is None or v > 0
        return v if self.it is None else self.it * per + v

    def seq(self):
        return self.b if self.it is None else self.it * 2 + self.b


class Slot:
    def __init__(self, t, it=None):
        self.t, self.it = t, it

    def once(self, offset):
        if (self.t - offset) % SLOTS:
            return None
        return self.chunk(offset)

    def chunk(self, offset):
        b, s = divmod(self.t - offset, SLOTS)
        if self.it is None and not 0 <= b < B:
            return None
        return Step(b, s, self.it)


def wait(eng, sem, value):
    if isinstance(value, int):
        if value > 0:
            eng.wait_ge(sem, value)
    else:
        eng.wait_ge(sem, value)


def run_slots(eng, slot):
    for t in range(LOOP_FROM):
        slot(Slot(t))
    with eng.Fori(0, LOOPS) as it:
        for t in range(BODY):
            slot(Slot(LOOP_FROM + t, it))
    for t in range(LOOP_FROM + BODY * LOOPS, LAST):
        slot(Slot(t))


def previous_use(slot, position, uses):
    for back in range(slot.t + 1):
        earlier = Slot(slot.t - back, slot.it)
        for use in sorted(uses, key=lambda u: -u[1]):
            st = earlier.once(use[0])
            if st and (back or use[1] < position):
                return st, use
    return None


def postln_layer(nc, x, Wqkv, bqkv, Wout, bout, w_gate_up, w_proj, out):
    ctx = ExitStack()
    with ctx:
        def sb(name, shape, dt=F32):
            return ctx.enter_context(nc.sbuf_tensor(name, shape, dt))

        def ps(name, shape, dt=F32):
            return ctx.enter_context(nc.psum_tensor(name, shape, dt))

        def sem(name):
            return ctx.enter_context(nc.semaphore(name))

        NGU = 2 * F // P
        wgu_raw = sb("wgu_raw", [P, NGU, D])
        wp_raw = sb("wp_raw", [P, DT, F])
        PW = 2 * D
        PG = PW // Q_GROUP
        w_bf = sb("w_bf", [P, 2, PG, Q_GROUP], BF16)
        w_abs = sb("w_abs", [P, 2, PG, Q_GROUP], BF16)
        w_sign = sb("w_sign", [P, 2, PG, Q_GROUP], BF16)
        w_hat = sb("w_hat", [P, 2, PG, Q_GROUP], BF16)
        w_sum = sb("w_sum", [P, PG])
        w_scale = sb("w_scale", [P, PG], BF16)
        w_half = sb("w_half", [P, PG], BF16)
        wguT = sb("wguT", [P, DT, 2 * F], F32R)
        wpT = sb("wpT", [P, FT, D], F32R)
        wqkv = sb("wqkv", [P, DT, D + 2 * KV])
        wqkv_p = [sb(f"wqkv_{n}", [P, DT, D + 2 * KV], F32R) for n in ("hi", "lo")]
        wv_p = sb("wv_p", [P, DT, 2, KV], F32R)
        wo = sb("wo", [P, DT, D])
        wo_p = [sb(f"wo_{n}", [P, DT, D], F32R) for n in ("hi", "lo")]
        bq = sb("bq", [P, DT])
        bq_s = sb("bq_s", [P, DT])
        bk = sb("bk", [KV, 1])
        bv = sb("bv", [P, KV])
        bo = sb("bo", [P, D])
        ident = sb("ident", [P, P])
        ident_bf = sb("ident_bf", [P, P], BF16)
        ones = sb("ones", [P, 1])
        minus_half = sb("minus_half", [P, TT])
        ln_eps = sb("ln_eps", [P, TT])

        xn = sb("xn", [P, 2, TT, D])
        xT = [sb(f"xT_{n}", [P, DT, S], F32R) for n in ("hi", "lo")]
        q_f = sb("q_f", [P, DT, S])
        q_p = sb("q_p", [P, 2, DT, S], F32R)
        k_f = sb("k_f", [KV, S])
        k_p = sb("k_p", [KV, 2, S], F32R)
        q_dram = nc.dram_tensor("q_dram", [2, 2, D, S], F32)
        k_dram = nc.dram_tensor("k_dram", [2, 2, KV, S], F32)
        SROWS = 4 * HD
        XROWS = SROWS + 2
        q_st = sb("q_st", [XROWS, 2, H, S], F32R)
        k_st = sb("k_st", [XROWS, 2, G, S], F32R)
        v_ones = sb("v_ones", [P, 2, TT, G, 2 * HD])
        v_f = sb("v_f", [P, TT, KV])
        row_max = sb("row_max", [P, 2, H * TT])
        shift_p = [[sb(f"shift{h}_{n}", [H * TT // 2, P], F32R) for n in ("hi", "lo")] for h in range(2)]
        probs = sb("probs", [P, 2, TT, 2, S])
        pv_sb = sb("pv_sb", [P, 2, S])
        den_r = sb("den_r", [P, 2 * TT * 4])
        att = sb("att", [P, TT, D])
        attT = [sb(f"attT_{n}", [P, DT, S], F32R) for n in ("hi", "lo")]
        res = sb("res", [P, 2, TT, D])
        r1 = sb("r1", [P, TT, D])
        st1 = sb("st1", [P, TT, 6])
        mv1 = sb("mv1", [P, TT, 2])
        ve1 = sb("ve1", [P, TT])
        rstd1 = sb("rstd1", [P, TT])
        x1 = sb("x1", [P, 2, TT, D])
        x1T = [sb(f"x1T_{n}", [P, 2, DT, S], F32R) for n in ("hi", "lo")]
        tanh = sb("tanh", [P, 2, S])
        gated = sb("gated", [P, 2, S])
        h_f = sb("h_f", [P, 2, S])
        h_p = [sb(f"h_{n}", [P, 2, S], F32R) for n in ("hi", "lo")]
        h_sq = sb("h_sq", [P, 2, S])
        sq_sum = sb("sq_sum", [P, 2, S])
        y_sb = sb("y_sb", [P, TT, D])
        ms = sb("ms", [P, TT])
        inv = sb("inv", [P, TT])
        r2 = sb("r2", [P, TT, D])
        st2 = sb("st2", [P, TT, 6])
        mv2 = sb("mv2", [P, TT, 2])
        ve2 = sb("ve2", [P, TT])
        rstd2 = sb("rstd2", [P, TT])
        y_out = sb("y_out", [P, 2, TT, D])

        max_ps = ps("max_ps", [P, TT, S])
        exp_ps = ps("exp_ps", [P, TT, 2 * S])
        ffn_ps = ps("ffn_ps", [P, 2, S])
        down_ps = ps("down_ps", [P, TT, D])
        pv_ps = ps("pv_ps", [P, 2, S])
        misc_ps = [ps(f"misc{i}_ps", [P, 512]) for i in range(2)]

        w_loaded = [sem(f"w_loaded{i}") for i in range(3)]
        consts_made, k_ones = sem("consts_made"), sem("k_ones")
        w_act, w_red, w_dve, w_tr, w_ev = sem("w_act"), sem("w_red"), sem("w_dve"), sem("w_tr"), sem("w_ev")
        w_pool = sem("w_pool")
        wo_loaded, wo_hi, wo_split = sem("wo_loaded"), sem("wo_hi"), sem("wo_split")
        w_split_hi, w_split = sem("w_split_hi"), sem("w_split")
        x_loaded = [sem(f"x_loaded{i}") for i in range(2)]
        res_loaded = [sem(f"res_loaded{i}") for i in range(2)]
        xT_made, xT_hi, xT_lo = sem("xT_made"), sem("xT_hi"), sem("xT_lo")
        q_made, q_copied, q_lo = sem("q_made"), sem("q_copied"), sem("q_lo")
        k_made, k_copied, k_lo = sem("k_made"), sem("k_copied"), sem("k_lo")
        v_made, v_biased, v_copied = sem("v_made"), sem("v_biased"), sem("v_copied")
        qk_saved = [sem(f"qk_saved{i}") for i in range(2)]
        qk_stacked = [sem(f"qk_stacked{i}") for i in range(2)]
        max_scored, max_taken = sem("max_scored"), sem("max_taken")
        shift_turned, shift_split = sem("shift_turned"), sem("shift_split")
        shift_hi = sem("shift_hi")
        shift_loaded = [sem(f"shift_loaded{i}") for i in range(2)]
        exp_scored, exp_done = sem("exp_scored"), sem("exp_done")
        pv_done, pv_copied, pv_turned = sem("pv_done"), sem("pv_copied"), sem("pv_turned")
        den_done, att_done = sem("den_done"), sem("att_done")
        att_turned, attT_hi, attT_lo = sem("att_turned"), sem("attT_hi"), sem("attT_lo")
        bout_added, o_made = sem("bout_added"), sem("o_made")
        r1_done, bn1_done, var1_done, ve1_done, rstd1_done, x1_done = (
            sem("r1_done"), sem("bn1_done"), sem("var1_done"), sem("ve1_done"), sem("rstd1_done"), sem("x1_done"))
        x1_turned, x1T_hi, x1T_lo = sem("x1_turned"), sem("x1T_hi"), sem("x1T_lo")
        ffn_made, tanh_done, gated_done, h_done = sem("ffn_made"), sem("tanh_done"), sem("gated_done"), sem("h_done")
        h_hi, h_squared, h_lo, h_summed = sem("h_hi"), sem("h_squared"), sem("h_lo"), sem("h_summed")
        down_done, y_copied, sq_summed, ms_done, inv_done = (
            sem("down_done"), sem("y_copied"), sem("sq_summed"), sem("ms_done"), sem("inv_done"))
        r2_done, bn2_done, var2_done, ve2_done, rstd2_done, y_done = (
            sem("r2_done"), sem("bn2_done"), sem("var2_done"), sem("ve2_done"), sem("rstd2_done"), sem("y_done"))
        waited, sp_waited = sem("waited"), sem("sp_waited")
        stored = [sem(f"stored{i}") for i in range(2)]

        pieces = []
        for r in range(0, NGU, 2):
            pieces.append((wgu_raw[:, r:r + 2, :], 1, [a * D + k * P for k in range(DT) for a in range(2)],
                           wguT[:, :, r * P:(r + 2) * P]))
        for k in range(0, FT, 2):
            pieces.append((wp_raw[:, :, k * P:(k + 2) * P], 2, [r * 2 * P + a * P for a in range(2) for r in range(DT)],
                           wpT[:, k:k + 2, :]))
        turn_banks = (ffn_ps, down_ps)

        def piece(n, first):
            return n.t - first if n.it is None and 0 <= n.t - first < len(pieces) else None

        block = ctx.enter_context(nc.Block())

        @block.sync
        def _(sp):
            sp.dma_start(xn[:, 0], x[0].rearrange("(t p) d -> p t d", p=P)).then_inc(x_loaded[0], 16)
            sp.dma_start(wqkv[:], Wqkv.rearrange("(t p) n -> p t n", p=P)).then_inc(w_loaded[0], 16)
            with nc.allow_non_contiguous_dma("bias columns"):
                sp.dma_start(bq[:], bqkv[0:D].rearrange("(t p) -> p t", p=P)).then_inc(w_loaded[0], 16)
                sp.dma_start(bk[:], bqkv[D:D + KV].rearrange("(p o) -> p o", o=1)).then_inc(w_loaded[0], 16)
            sp.dma_start(bv[:], bqkv[D + KV:D + 2 * KV].partition_broadcast(P)).then_inc(w_loaded[0], 16)
            sp.dma_start(wgu_raw[:], w_gate_up.rearrange("(t p) d -> p t d", p=P)).then_inc(w_loaded[1], 16)
            sp.dma_start(wp_raw[:], w_proj.rearrange("(t p) d -> p t d", p=P)).then_inc(w_loaded[2], 16)

            def sp_wait(semaphore, value):
                wait(sp, semaphore, value)
                if not isinstance(value, int):
                    sp.sem_inc(sp_waited, 1)

            def slot(n):
                if n.it is None and n.t == STACK_QK + 1:
                    for g in range(G):
                        for i in range(2):
                            at, row = 64 * (g // 2) + HD * quadrant(g, i), HD * (g + 4 * i)
                            sp.dma_start(wo[at:at + HD], Wout.rearrange("(h r) n -> r h n", h=2)[row:row + HD]
                                         ).then_inc(wo_loaded, 16)
                    sp.dma_start(bo[:], bout.partition_broadcast(P)).then_inc(wo_loaded, 16)
                for half in range(2):
                    if st := n.once(SHIFT_T[half]):
                        sp_wait(shift_split, st.count(2, half + 1))
                        for part in range(2):
                            sp.dma_start(
                                q_st[SROWS + part:SROWS + part + 1, st.par, half * H // 2:(half + 1) * H // 2, :]
                                .bitcast(F32), shift_p[half][part][:].bitcast(F32)).then_inc(shift_loaded[half], 16)
                if st := n.once(SAVE_QK):
                    sp_wait(q_lo, st.count(1, 1))
                    sp_wait(k_lo, st.count(1, 1))
                    sp_wait(qk_stacked[st.par], st.count2(128, 0))
                    sp.dma_start(q_dram[st.par].rearrange("a (m p) t -> p a m t", p=P), q_p[:].bitcast(F32)
                                 ).then_inc(qk_saved[st.par], 16)
                    sp.dma_start(k_dram[st.par].rearrange("a p t -> p a t"), k_p[:].bitcast(F32)
                                 ).then_inc(qk_saved[st.par], 16)
                if st := n.once(STACK_QK):
                    sp_wait(qk_saved[st.par], st.count2(32, 32))
                    sp_wait(exp_scored, st.count(8, -8))
                    for c in range(4):
                        sp.dma_start(
                            k_st[c * HD:(c + 1) * HD, st.par].bitcast(F32),
                            k_dram[st.par, c % 2].rearrange("(g d) t -> d g t", d=HD)).then_inc(qk_stacked[st.par], 16)
                        sp.dma_start(
                            q_st[c * HD:(c + 1) * HD, st.par].bitcast(F32),
                            q_dram[st.par, c // 2].rearrange("(h d) t -> d h t", d=HD)
                        ).then_inc(qk_stacked[st.par], 16)
                if (st := n.once(LOAD_X)) and not (st.it is None and st.b == 0):
                    sp_wait(xT_made, st.count(1, -1))
                    sp.dma_start(xn[:, st.par], x[st.seq()].rearrange("(t p) d -> p t d", p=P)
                                 ).then_inc(x_loaded[st.par], 16)
                if st := n.once(LOAD_RES):
                    sp_wait(r1_done, st.count(1, -1))
                    sp.dma_start(res[:, st.par], x[st.seq()].rearrange("(t p) d -> p t d", p=P)
                                 ).then_inc(res_loaded[st.par], 16)
                if st := n.once(STORE):
                    sp_wait(y_done, st.count(TT, TT))
                    sp.dma_start(out[st.seq()].rearrange("(t p) d -> p t d", p=P), y_out[:, st.par]
                                 ).then_inc(stored[st.par], 16)

            run_slots(sp, slot)
            for i in range(2):
                sp.wait_ge(stored[i], 16 * B // 2)

        @block.tensor
        def _(pe):
            def products(dst, lhs, rhs, start=True, stop=True):
                pairs = list(zip(lhs, rhs))
                for i, (a, b) in enumerate(pairs):
                    last = pe.matmul(dst, a, b, start=start and i == 0, stop=stop and i == len(pairs) - 1)
                return last

            pe.wait_ge(consts_made, 3)

            def turn_weights(c):
                pe.wait_ge(w_pool, 2 * (c + 1))
                if c >= 2:
                    pe.wait_ge(w_ev, c - 1)
                flat = w_hat[:, c % 2].rearrange("p g e -> p (g e)")
                for i, at in enumerate(pieces[c][2]):
                    last = pe.transpose(turn_banks[c % 2][:].rearrange("p a b -> p (a b)").bitcast(BF16)[:, i * P:(i + 1) * P],
                                        flat[:, at:at + P], ident_bf[:])
                last.then_inc(w_tr, 1)

            misc_users = [
                [(PROJ_V, 0, v_copied, 1, 1), (X_T, 0, xT_lo, 1, 1), (PROJ_Q, 0, q_copied, 1, 1),
                 (SHIFT_T[0], 0, shift_split, 2, 1), (PV_T[0], 0, att_done, 4, 2), (PV_T[1], 0, att_done, 4, 4)],
                [(ATT_T, 0, attT_lo, 1, 1), (PROJ_O, 0, r1_done, 1, 1), (PROJ_K, 0, k_copied, 1, 1),
                 (X1_T, 0, x1T_lo, 1, 1), (SUM_SQ, 0, ms_done, 1, 1), (SHIFT_T[1], 0, shift_split, 2, 2)]]

            def use_misc(n, bank):
                if found := previous_use(n, 0, misc_users[bank]):
                    st, (_, _, released, per, extra) = found
                    wait(pe, released, st.count(per, extra))

            def max_scores(st, i):
                if i == 0:
                    wait(pe, qk_stacked[st.par], st.count2(128, 128))
                wait(pe, max_taken, st.count(16, 2 * st.s + i))
                head = first_head(st.s) + 4 * i
                for t in range(TT):
                    last = pe.matmul(max_ps[:, t, :], q_st[0:SROWS, st.par, head, t * P:(t + 1) * P],
                                     k_st[0:SROWS, st.par, st.s % 4, :], start=True, stop=True)
                last.then_inc(max_scored, 1)

            def exp_scores(st):
                wait(pe, shift_loaded[st.s // 4], st.count(32, 32))
                wait(pe, exp_done, st.count(8, st.s))
                for t in range(TT):
                    last = pe.matmul(exp_ps[:, t, :], k_st[:, st.par, st.s % 4, t * P:(t + 1) * P],
                                     q_st[:, st.par, first_head(st.s):first_head(st.s) + 5:4, :], start=True, stop=True)
                last.then_inc(exp_scored, 1)

            def gate_up(st):
                wait(pe, x1T_lo, st.count(1, 1))
                if st.it is None and st.b == 0 and st.s == 0:
                    pe.wait_ge(w_ev, len(pieces))
                wait(pe, h_done, st.count(8, st.s))
                for half in range(2):
                    c = half * F + st.s * P
                    last = products(ffn_ps[:, half, :],
                                    [wguT[:, k, c:c + P] for k in range(DT) for _ in range(2)],
                                    [x1T[a][:, st.par, k, :] for k in range(DT) for a in range(2)])
                last.then_inc(ffn_made, 1)

            def down(st):
                wait(pe, h_lo, st.count(8, st.s + 1))
                wait(pe, h_hi, st.count(8, st.s + 1))
                if st.s == 0:
                    wait(pe, y_copied, st.count(1, 0))
                for t in range(TT):
                    for a in range(2):
                        last = pe.matmul(down_ps[:, t, :], h_p[a][:, st.s % 2, t * P:(t + 1) * P], wpT[:, st.s, :],
                                         start=(st.s == 0 and t == 0 and a == 0), stop=(st.s == FT - 1 and a == 1),
                                         skip_group_check=True)
                last.then_inc(down_done, 1)

            def times_v(st):
                wait(pe, exp_done, st.count(8, st.s + 1))
                wait(pe, v_copied, st.count(1, 1))
                if st.s % 4 == 0:
                    wait(pe, pv_copied, st.count(2, st.s // 4))
                g = st.s % 4
                for t in range(TT):
                    for i in range(2):
                        r = 32 * quadrant(g, i)
                        last = pe.matmul(pv_ps[r:r + 32, g // 2, :], v_ones[:, st.par, t, g, :],
                                         probs[:, st.s % 2, t, i, :], start=(t == 0), stop=(t == TT - 1),
                                         tile_position=(0, r))
                last.then_inc(pv_done, 1)

            def turn(bank, src, done):
                for i, blk in enumerate(src):
                    last = pe.transpose(misc_ps[bank][:, i * P:(i + 1) * P], blk, ident[:])
                last.then_inc(done, 1)

            def turn_maxima(st, half):
                wait(pe, max_taken, st.count(16, 8 * half + 8))
                pe.transpose(misc_ps[half][0:H * TT // 2, 0:P], row_max[:, st.par, half * H:(half + 1) * H], ident[:]
                             ).then_inc(shift_turned, 1)

            def slot(n):
                if st := n.chunk(MAX0):
                    if st.it is None and st.b == 0 and st.s == 0:
                        pe.wait_ge(k_ones, 1)
                    max_scores(st, 0)
                if st := n.chunk(EXP0):
                    exp_scores(st)
                if st := n.chunk(FFN0):
                    gate_up(st)
                if st := n.once(PROJ_V):
                    use_misc(n, 0)
                    wait(pe, xT_lo, st.count(1, 1))
                    for t in range(TT):
                        last = products(misc_ps[0][:, t * 2 * KV:(t + 1) * 2 * KV],
                                        [xT[a][:, k, t * P:(t + 1) * P] for k in range(DT) for a in range(2)],
                                        [wv_p[:, k] for k in range(DT) for _ in range(2)])
                    last.then_inc(v_made, 1)
                if st := n.once(X_T):
                    use_misc(n, 0)
                    wait(pe, x_loaded[st.par], st.count2(16, 16))
                    turn(0, [xn[:, st.par, t, k * P:(k + 1) * P] for k in range(DT) for t in range(TT)], xT_made)
                if st := n.once(PROJ_Q):
                    use_misc(n, 0)
                    wait(pe, xT_lo, st.count(1, 1))
                    wait(pe, w_split, 1)
                    for m in range(DT):
                        last = products(misc_ps[0][:, m * S:(m + 1) * S],
                                        [wqkv_p[c][:, k, m * P:(m + 1) * P] for k in range(DT) for c in range(2) for _ in range(2)],
                                        [xT[a][:, k, :] for k in range(DT) for _ in range(2) for a in range(2)])
                    last.then_inc(q_made, 1)
                if st := n.once(SHIFT_T[0]):
                    use_misc(n, 0)
                    turn_maxima(st, 0)
                for half in range(2):
                    if st := n.once(PV_T[half]):
                        use_misc(n, 0)
                        wait(pe, pv_copied, st.count(2, half + 1))
                        turn(0, [pv_sb[:, g, t * P:(t + 1) * P] for g in range(2) for t in range(TT)], pv_turned)
                if st := n.chunk(MAX0):
                    max_scores(st, 1)
                if st := n.chunk(PV0):
                    times_v(st)
                if st := n.once(ATT_T):
                    use_misc(n, 1)
                    wait(pe, att_done, st.count(4, 4))
                    turn(1, [att[:, t, m * P:(m + 1) * P] for m in range(DT) for t in range(TT)], att_turned)
                if st := n.once(PROJ_O):
                    use_misc(n, 1)
                    wait(pe, attT_lo, st.count(1, 1))
                    wait(pe, wo_split, 1)
                    for t in range(TT):
                        last = products(misc_ps[1][:, t * D:(t + 1) * D],
                                        [attT[a][:, m, t * P:(t + 1) * P] for m in range(DT) for a in range(2) for _ in range(2)],
                                        [wo_p[c][:, m, :] for m in range(DT) for _ in range(2) for c in range(2)])
                    last.then_inc(o_made, 1)
                if st := n.once(PROJ_K):
                    use_misc(n, 1)
                    last = products(misc_ps[1][0:KV, 0:S],
                                    [wqkv_p[c][:, k, D:D + KV] for k in range(DT) for c in range(2) for _ in range(2)],
                                    [xT[a][:, k, :] for k in range(DT) for _ in range(2) for a in range(2)])
                    last.then_inc(k_made, 1)
                if st := n.once(X1_T):
                    use_misc(n, 1)
                    wait(pe, x1_done, st.count(TT, TT))
                    turn(1, [x1[:, st.par, t, k * P:(k + 1) * P] for k in range(DT) for t in range(TT)], x1_turned)
                if st := n.once(SUM_SQ):
                    use_misc(n, 1)
                    wait(pe, h_summed, st.count(FT - 1, FT - 1))
                    for t in range(TT):
                        last = pe.matmul(misc_ps[1][:, t:t + 1], sq_sum[:, st.par, t * P:(t + 1) * P], ones[:],
                                         start=True, stop=True)
                    last.then_inc(sq_summed, 1)
                if st := n.once(SHIFT_T[1]):
                    use_misc(n, 1)
                    turn_maxima(st, 1)
                if st := n.chunk(DOWN0):
                    down(st)
                if (c := piece(n, TURN_W0)) is not None:
                    turn_weights(c)

            run_slots(pe, slot)

        @block.scalar
        def _(act):
            act.wait_ge(w_loaded[0], 16 * 4)
            act.activation(wqkv_p[0][:], wqkv[:], ACT.Identity).then_inc(w_split_hi, 1)
            act.activation(bq_s[:], bq[:], ACT.Identity, scale=1.0 / HD).then_inc(w_split_hi, 1)
            act.activation(wv_p[:, :, 0, :], wqkv[:, :, D + KV:], ACT.Identity).then_inc(w_split_hi, 1)
            act.wait_ge(w_split_hi, 3)

            def read_weights(c):
                raw, load = pieces[c][0:2]
                act.wait_ge(w_loaded[load], 16)
                if c >= 2:
                    act.wait_ge(w_pool, 2 * (c - 1))
                flat = w_bf[:, c % 2].rearrange("p g e -> p (g e)")
                act.activation(flat.rearrange("p (a b) -> p a b", a=2), raw, ACT.Identity).then_inc(w_act, 1)
                act.wait_ge(w_act, 3 * c + 1)
                act.activation(w_abs[:, c % 2].rearrange("p g e -> p (g e)"), flat, ACT.Abs).then_inc(w_act, 1)
                act.activation(w_sign[:, c % 2].rearrange("p g e -> p (g e)"), flat, ACT.Sign).then_inc(w_act, 1)

            def high(dst, src):
                return act.activation(dst, src, ACT.Identity)

            def both(bank):
                return misc_ps[bank][:].rearrange("p (k t) -> p k t", k=2)

            def slot(n):
                if st := n.chunk(EXP0):
                    wait(act, exp_scored, st.count(8, st.s + 1))
                    wait(act, pv_done, st.count(8, st.s - 1))
                    act.activation(probs[:, st.s % 2], exp_ps[:], ACT.Exp).then_inc(exp_done, 1)
                if st := n.chunk(FFN0):
                    wait(act, ffn_made, st.count(8, st.s + 1))
                    wait(act, gated_done, st.count(8, st.s - 1))
                    act.activation(tanh[:, st.s % 2, :], ffn_ps[:, 0, :], ACT.Tanh, scale=0.5).then_inc(tanh_done, 1)
                if st := n.once(X_T):
                    wait(act, xT_made, st.count(1, 1))
                    wait(act, v_made, st.count(1, 0))
                    high(xT[0][:], both(0)).then_inc(xT_hi, 1)
                if st := n.once(PROJ_Q):
                    wait(act, q_made, st.count(1, 1))
                    wait(act, q_lo, st.count(1, 0))
                    if st.it is not None or st.b > 0:
                        wait(act, qk_saved[1 - st.par], Step(st.b - 1, 0, st.it).count2(32, 32))
                    for m in range(DT):
                        for dst in (q_f[:, m, :], q_p[:, 0, m, :]):
                            last = act.activation(dst, misc_ps[0][:, m * S:(m + 1) * S], ACT.Identity,
                                                  bias=bq_s[:, m:m + 1], scale=1.0 / HD)
                    last.then_inc(q_copied, 1)
                if st := n.chunk(FFN0):
                    wait(act, h_done, st.count(8, st.s + 1))
                    wait(act, down_done, st.count(8, st.s - 1))
                    high(h_p[0][:, st.s % 2, :], h_f[:, st.s % 2, :]).then_inc(h_hi, 1)
                    if st.s == 0:
                        wait(act, sq_summed, st.count(1, -1))
                        dst = sq_sum[:, st.par, :]
                    else:
                        wait(act, h_summed, st.count(FT - 1, max(st.s - 2, 0)))
                        dst = h_sq[:, st.s % 2, :]
                    act.activation(dst, h_f[:, st.s % 2, :], ACT.Square).then_inc(h_squared, 1)
                for half in range(2):
                    if st := n.once(PV_COPY[half]):
                        wait(act, pv_done, st.count(8, 4 * half + 4))
                        wait(act, pv_turned, st.count(2, half))
                        act.activation(pv_sb[:], pv_ps[:], ACT.Identity).then_inc(pv_copied, 1)
                if st := n.once(X1_T):
                    wait(act, x1_turned, st.count(1, 1))
                    wait(act, ffn_made, st.count(8, -8))
                    high(x1T[0][:, st.par], both(1)).then_inc(x1T_hi, 1)
                if st := n.once(ATT_T):
                    wait(act, att_turned, st.count(1, 1))
                    wait(act, o_made, st.count(1, 0))
                    high(attT[0][:], both(1)).then_inc(attT_hi, 1)
                if st := n.once(PROJ_K):
                    wait(act, k_made, st.count(1, 1))
                    wait(act, k_lo, st.count(1, 0))
                    for dst in (k_f[:], k_p[:, 0, :]):
                        last = act.activation(dst, misc_ps[1][0:KV, 0:S], ACT.Identity, bias=bk[:, 0:1])
                    last.then_inc(k_copied, 1)
                if st := n.once(Y_COPY):
                    wait(act, down_done, st.count(8, 8))
                    wait(act, r2_done, st.count(TT, 0))
                    act.activation(y_sb[:], down_ps[:], ACT.Identity).then_inc(y_copied, 1)
                if (c := piece(n, READ_W0)) is not None:
                    read_weights(c)
                if n.it is None and n.t == WO_SPLIT:
                    act.wait_ge(wo_loaded, 16 * (2 * G + 1))
                    act.activation(wo_p[0][:], wo[:], ACT.Identity).then_inc(wo_hi, 1)

            run_slots(act, slot)

        @block.vector
        def _(dve):
            dve.memset(k_st[SROWS:XROWS].bitcast(F32), 1.0).then_inc(k_ones, 1)
            dve.wait_ge(w_split_hi, 3)
            dve.tensor_tensor(wqkv_p[1][:], wqkv[:], wqkv_p[0][:].bitcast(F32), ALU.subtract)
            dve.tensor_tensor(wv_p[:, :, 1, :], wqkv[:, :, D + KV:], wqkv_p[0][:, :, D + KV:].bitcast(F32), ALU.subtract
                              ).then_inc(w_split, 1)

            def low(dst, src, hi):
                return dve.tensor_tensor(dst, src, hi.bitcast(F32), ALU.subtract)

            def both(bank):
                return misc_ps[bank][:].rearrange("p (k t) -> p k t", k=2)

            def take_maximum(st, i):
                wait(dve, max_scored, st.count(16, 2 * st.s + i + 1))
                if st.s == 0 and i == 0:
                    wait(dve, shift_turned, st.count(2, -2))
                head = first_head(st.s) + 4 * i
                dve.tensor_reduce(row_max[:, st.par, head * TT:(head + 1) * TT], max_ps[:], AX.X, ALU.max
                                  ).then_inc(max_taken, 1)

            def shift_rows(st, half):
                src = misc_ps[half][0:H * TT // 2, 0:P]
                hi, lo = shift_p[half]
                wait(dve, shift_turned, st.count(2, half + 1))
                wait(dve, shift_loaded[half], st.count(32, 0))
                dve.tensor_scalar(hi[:], src, -1.0, None, ALU.mult).then_inc(shift_hi, 1)
                wait(dve, shift_hi, st.count(2, half + 1))
                dve.scalar_tensor_tensor(lo[:], src, -1.0, hi[:].bitcast(F32), ALU.mult, ALU.subtract
                                         ).then_inc(shift_split, 1)

            def tern_weights(c):
                dve.wait_ge(w_act, 3 * c + 3)
                dve.tensor_reduce(w_sum[:], w_abs[:, c % 2], AX.X, ALU.add).then_inc(w_red, 1)
                dve.wait_ge(w_red, 3 * c + 1)
                dve.tensor_scalar(w_scale[:], w_sum[:], 1.0 / Q_GROUP, 1e-8, ALU.mult, ALU.max).then_inc(w_red, 1)
                dve.wait_ge(w_red, 3 * c + 2)
                dve.tensor_scalar(w_half[:], w_scale[:], 0.5, None, ALU.mult).then_inc(w_red, 1)
                dve.wait_ge(w_red, 3 * c + 3)
                if c >= 2:
                    dve.wait_ge(w_tr, c - 1)
                half = w_half[:].unsqueeze(2).broadcast_to([P, PG, Q_GROUP])
                scale = w_scale[:].unsqueeze(2).broadcast_to([P, PG, Q_GROUP])
                hat = w_hat[:, c % 2]
                for i, (a, b, op) in enumerate(((w_abs[:, c % 2], half, ALU.is_gt), (hat, scale, ALU.mult),
                                                (hat, w_sign[:, c % 2], ALU.mult))):
                    if i:
                        dve.wait_ge(w_dve, 3 * c + i)
                    dve.tensor_tensor(hat, a, b, op).then_inc(w_dve, 1)

            def slot(n):
                if st := n.chunk(MAX0):
                    take_maximum(st, 0)
                if st := n.chunk(FFN0):
                    wait(dve, tanh_done, st.count(8, st.s + 1))
                    dve.scalar_tensor_tensor(gated[:, st.s % 2, :], tanh[:, st.s % 2, :], 1.0, ffn_ps[:, 0, :],
                                             ALU.add, ALU.mult).then_inc(gated_done, 1)
                    wait(dve, gated_done, st.count(8, st.s + 1))
                    wait(dve, h_lo, st.count(8, st.s - 1))
                    wait(dve, h_squared, st.count(8, st.s - 1))
                    dve.tensor_tensor(h_f[:, st.s % 2, :], gated[:, st.s % 2, :], ffn_ps[:, 1, :], ALU.mult
                                      ).then_inc(h_done, 1)
                if st := n.once(PROJ_V):
                    wait(dve, v_made, st.count(1, 1))
                    v = misc_ps[0][:, 0:TT * 2 * KV].rearrange("p (t c n) -> p t c n", t=TT, c=2)
                    for t in range(TT):
                        dve.tensor_tensor(v_f[:, t, :], v[:, t, 0, :], bv[:], ALU.add).then_inc(v_biased, 1)
                    wait(dve, v_biased, st.count(TT, TT))
                    wait(dve, pv_done, st.count(8, -8))
                    for t in range(TT):
                        last = dve.tensor_tensor(
                            v_ones[:, st.par, t, :, 0:HD], v_f[:, t, :].rearrange("p (g d) -> p g d", g=G),
                            v[:, t, 1, :].rearrange("p (g d) -> p g d", g=G), ALU.add)
                    last.then_inc(v_copied, 1)
                if st := n.once(X_T):
                    wait(dve, xT_hi, st.count(1, 1))
                    low(xT[1][:], both(0), xT[0][:]).then_inc(xT_lo, 1)
                if st := n.once(SHIFT_T[0]):
                    shift_rows(st, 0)
                for half in range(2):
                    if st := n.once(PV_T[half]):
                        pv = misc_ps[0][:].rearrange("p (g t j e) -> p g t j e", g=2, t=TT, j=4)
                        rec = den_r[:].rearrange("p (g t j) -> p g t j", g=2, t=TT)
                        wait(dve, pv_turned, st.count(2, half + 1))
                        wait(dve, att_done, st.count(4, 2 * half))
                        dve.reciprocal(rec.rearrange("p g t j -> p (g t) j"),
                                       pv.rearrange("p g t j e -> p (g t) j e")[:, :, :, HD]).then_inc(den_done, 1)
                        wait(dve, den_done, st.count(2, half + 1))
                        if half == 0:
                            wait(dve, att_turned, st.count(1, 0))
                        for i in range(2):
                            dve.tensor_tensor(
                                att[:].rearrange("p t (h i j d) -> p t h i j d", h=2, i=2, j=4)[:, :, half, i],
                                pv[:, i, :, :, 0:HD],
                                rec[:, i].unsqueeze(3).broadcast_to([P, TT, 4, HD]), ALU.mult).then_inc(att_done, 1)
                if st := n.chunk(MAX0):
                    take_maximum(st, 1)
                if st := n.once(PROJ_K):
                    wait(dve, k_copied, st.count(1, 1))
                    low(k_p[:, 1, :], k_f[:], k_p[:, 0, :]).then_inc(k_lo, 1)
                if st := n.once(SHIFT_T[1]):
                    shift_rows(st, 1)
                if st := n.once(SUM_SQ):
                    wait(dve, sq_summed, st.count(1, 1))
                    dve.tensor_scalar(ms[:], misc_ps[1][:, 0:TT], 1.0 / F, 4.0 * RMS_EPS, ALU.mult, ALU.add
                                      ).then_inc(ms_done, 1)
                if st := n.once(ATT_T):
                    wait(dve, attT_hi, st.count(1, 1))
                    low(attT[1][:], both(1), attT[0][:]).then_inc(attT_lo, 1)
                if st := n.once(PROJ_O):
                    wait(dve, o_made, st.count(1, 1))
                    wait(dve, bout_added, st.count(1, 1))
                    dve.tensor_tensor(r1[:], both(1), res[:, st.par], ALU.add).then_inc(r1_done, 1)
                    wait(dve, r1_done, st.count(1, 1))
                    for t in range(TT):
                        dve.bn_stats(st1[:, t, :], r1[:, t, :]).then_inc(bn1_done, 1)
                    wait(dve, bn1_done, st.count(TT, TT))
                    dve.sem_inc(waited, 1)
                    for t in range(TT):
                        dve.bn_aggr(mv1[:, t, :], st1[:, t, :]).then_inc(var1_done, 1)
                if st := n.once(X1_T):
                    wait(dve, x1T_hi, st.count(1, 1))
                    low(x1T[1][:, st.par], both(1), x1T[0][:, st.par]).then_inc(x1T_lo, 1)
                if st := n.once(LN1_APPLY):
                    wait(dve, rstd1_done, st.count(1, 1))
                    for t in range(TT):
                        dve.tensor_scalar(x1[:, st.par, t, :], r1[:, t, :], mv1[:, t, 0:1], rstd1[:, t:t + 1],
                                          ALU.subtract, ALU.mult).then_inc(x1_done, 1)
                if st := n.once(LN2_STATS):
                    wait(dve, inv_done, st.count(1, 1))
                    wait(dve, y_copied, st.count(1, 1))
                    for t in range(TT):
                        dve.scalar_tensor_tensor(r2[:, t, :], y_sb[:, t, :], inv[:, t:t + 1], x1[:, st.par, t, :],
                                                 ALU.mult, ALU.add).then_inc(r2_done, 1)
                    for t in range(TT):
                        wait(dve, r2_done, st.count(TT, t + 1))
                        dve.bn_stats(st2[:, t, :], r2[:, t, :]).then_inc(bn2_done, 1)
                    wait(dve, bn2_done, st.count(TT, TT))
                    dve.sem_inc(waited, 1)
                    for t in range(TT):
                        dve.bn_aggr(mv2[:, t, :], st2[:, t, :]).then_inc(var2_done, 1)
                if st := n.once(LN2_APPLY):
                    wait(dve, rstd2_done, st.count(1, 1))
                    wait(dve, stored[st.par], st.count2(16, 0))
                    for t in range(TT):
                        dve.tensor_scalar(y_out[:, st.par, t, :], r2[:, t, :], mv2[:, t, 0:1], rstd2[:, t:t + 1],
                                          ALU.subtract, ALU.mult).then_inc(y_done, 1)
                if (c := piece(n, READ_W0)) is not None:
                    tern_weights(c)
                if (c := piece(n, TURN_W0)) is not None:
                    dve.wait_ge(w_tr, c + 1)
                    dve.tensor_copy(pieces[c][3], turn_banks[c % 2][:].rearrange("p a b -> p (a b)").bitcast(BF16)[:, 0:4 * P]
                                    .rearrange("p (k t) -> p k t", k=2)).then_inc(w_ev, 1)
                if n.it is None and n.t == WO_SPLIT:
                    dve.wait_ge(wo_hi, 1)
                    dve.tensor_tensor(wo_p[1][:], wo[:], wo_p[0][:].bitcast(F32), ALU.subtract).then_inc(wo_split, 1)

            run_slots(dve, slot)

        @block.gpsimd
        def _(pool):
            pool.memset(ident[:], 0.0).then_inc(consts_made, 1)
            pool.memset(ones[:], 1.0)
            pool.memset(minus_half[:], -0.5)
            pool.memset(ln_eps[:], LN_EPS)
            pool.memset(v_ones[:], 1.0)
            pool.wait_ge(consts_made, 1)
            pool.affine_select(out=ident[:], in_=ident[:], compare_op=ALU.not_equal, fill=1.0, base=0,
                               pattern=[[-1, P]], channel_multiplier=1).then_inc(consts_made, 1)
            pool.wait_ge(consts_made, 2)
            pool.tensor_copy(ident_bf[:], ident[:]).then_inc(consts_made, 1)

            def rsqrt(dst, src, done):
                pool.tensor_tensor(dst, src, minus_half[:], ALU.pow).then_inc(done, 1)

            def slot(n):
                if st := n.chunk(FFN0):
                    wait(pool, h_hi, st.count(8, st.s + 1))
                    wait(pool, down_done, st.count(8, st.s - 1))
                    pool.tensor_tensor(h_p[1][:, st.s % 2, :], h_f[:, st.s % 2, :],
                                       h_p[0][:, st.s % 2, :].bitcast(F32), ALU.subtract).then_inc(h_lo, 1)
                    if st.s:
                        wait(pool, h_squared, st.count(8, st.s + 1))
                        wait(pool, h_summed, st.count(FT - 1, st.s - 1))
                        pool.tensor_tensor(sq_sum[:, st.par, :], sq_sum[:, st.par, :], h_sq[:, st.s % 2, :], ALU.add
                                           ).then_inc(h_summed, 1)
                if st := n.once(PROJ_Q):
                    wait(pool, q_copied, st.count(1, 1))
                    pool.tensor_tensor(q_p[:, 1], q_f[:], q_p[:, 0].bitcast(F32), ALU.subtract).then_inc(q_lo, 1)
                if (c := piece(n, READ_W0)) is not None:
                    pool.wait_ge(w_dve, 3 * (c + 1))
                    hat = w_hat[:, c % 2]
                    pool.tensor_tensor(hat, hat, w_bf[:, c % 2], ALU.subtract).then_inc(w_pool, 1)
                    pool.wait_ge(w_pool, 2 * c + 1)
                    pool.tensor_tensor(hat, hat, w_bf[:, c % 2], ALU.add).then_inc(w_pool, 1)
                if st := n.once(ADD_BOUT):
                    if st.it is None and st.b == 0:
                        pool.wait_ge(wo_loaded, 16 * (2 * G + 1))
                    wait(pool, res_loaded[st.par], st.count2(16, 16))
                    for t in range(TT):
                        last = pool.tensor_tensor(res[:, st.par, t, :], res[:, st.par, t, :], bo[:], ALU.add)
                    last.then_inc(bout_added, 1)
                if st := n.once(PROJ_O):
                    wait(pool, var1_done, st.count(TT, TT))
                    pool.tensor_tensor(ve1[:], mv1[:, :, 1], ln_eps[:], ALU.add).then_inc(ve1_done, 1)
                    wait(pool, ve1_done, st.count(1, 1))
                    rsqrt(rstd1[:], ve1[:], rstd1_done)
                if st := n.once(SUM_SQ):
                    wait(pool, ms_done, st.count(1, 1))
                    rsqrt(inv[:], ms[:], inv_done)
                if st := n.once(LN2_STATS):
                    wait(pool, var2_done, st.count(TT, TT))
                    pool.tensor_tensor(ve2[:], mv2[:, :, 1], ln_eps[:], ALU.add).then_inc(ve2_done, 1)
                    wait(pool, ve2_done, st.count(1, 1))
                    rsqrt(rstd2[:], ve2[:], rstd2_done)

            run_slots(pool, slot)


_INS = ["L0_attn_x", "L0_attn_Wqkv", "L0_attn_bqkv", "L0_attn_Wout", "L0_attn_bout", "L0_ffn_w_gate_up",
        "L0_ffn_w_proj"]


def kernel(**inputs):
    import numpy as _np
    import concourse.bacc as _bacc
    from concourse import mybir as _mybir
    from concourse.bass_utils import run_bass_kernel_spmd as _run

    nc = _bacc.Bacc("TRN2", target_bir_lowering=False, num_devices=1)
    arrays, args = {}, []
    for name in _INS:
        a = _np.ascontiguousarray(inputs[name])
        arrays[f"in_{name}_dram"] = a
        args.append(nc.dram_tensor(f"in_{name}_dram", a.shape, _mybir.dt.from_np(a.dtype), kind="ExternalInput").ap())
    out = nc.dram_tensor("out_0_dram", (B, S, D), _mybir.dt.float32, kind="ExternalOutput").ap()
    postln_layer(nc, *args, out)
    r = _run(nc, [arrays], core_ids=[0])
    return r.results[0]["out_0_dram"]
```

```python
from contextlib import ExitStack

import concourse.bass as bass
from concourse import mybir

ALU = mybir.AluOpType
ACT = mybir.ActivationFunctionType
AX = mybir.AxisListType
F32 = mybir.dt.float32
F32R = mybir.dt.float32r
BF16 = mybir.dt.bfloat16

P = 128
B, S, D = 16, 256, 256
H, G, HD = 16, 4, 16
KV = G * HD
F = 4 * D
TT = S // P
DT = D // P
FT = F // P
Q_GROUP = 64
LN_EPS = 1e-5
RMS_EPS = 2.0 ** -23

SLOTS = 8
LOAD_X = 0
X_T = 1
PROJ_Q = 2
PROJ_K = 2
SAVE_QK = 2
STACK_QK = 3
MAX0 = 7
PROJ_V = 8
SHIFT_T = (11, 15)
EXP0 = 13
PV0 = 14
PV_COPY = (17, 21)
PV_T = (20, 22)
LOAD_RES = 21
ADD_BOUT = 23
ATT_T = 24
PROJ_O = 25
LN1_APPLY = 26
X1_T = 27
FFN0 = 29
DOWN0 = 30
Y_COPY = 37
SUM_SQ = 37
LN2_STATS = 38
LN2_APPLY = 39
STORE = 40
X_HIGH = 1
X_LOW = 1
Q_COPY = 2
Q_LOW = 2
K_COPY = 2
K_LOW = 2
V_COPY = 8
SHIFT_SPLIT = (11, 15)
PV_DIVIDE = (20, 22)
ATT_HIGH = 24
ATT_LOW = 24
O_ADD = 25
RSTD1 = 25
X1_HIGH = 27
X1_LOW = 27
GATE0 = 29
H0 = 29
H_HIGH0 = 29
H_LOW0 = 29
MEAN_SQ = 37
INV = 37
RSTD2 = 38
SHORT_ORDER = ("max0", "x1", "x", "v", "shift0", "q", "pv0", "pv1", "max1", "o", "k", "att", "shift1", "sq")
SHORT_OFFSET = {"v": PROJ_V, "x": X_T, "q": PROJ_Q, "shift0": SHIFT_T[0], "shift1": SHIFT_T[1], "pv0": PV_T[0],
                "pv1": PV_T[1], "o": PROJ_O, "att": ATT_T, "k": PROJ_K, "x1": X1_T, "sq": SUM_SQ}
SHORT_USES = [(m, name) for m in range(SLOTS) for name in SHORT_ORDER
              if name not in SHORT_OFFSET or SHORT_OFFSET[name] % SLOTS == m]
BANK_TURNS = (0, 1, 2) * 8 + (0, 1, 0, 2)
BANKS_FROM = 0
assert len(SHORT_USES) == len(BANK_TURNS)
BANK = {use: BANK_TURNS[(i + BANKS_FROM) % len(BANK_TURNS)] for i, use in enumerate(SHORT_USES)}
W_READ = (2, 3, 4, 5, 6, 8, 10, 12, 14, 16, 18, 20)
W_MAKE, W_TURN, W_PLACE = 1, 3, 4
WO_SPLIT = 14

LAST = SLOTS * B + STORE
LOOP_FROM, BODY = 48, 2 * SLOTS
LOOPS = (SLOTS * B - LOOP_FROM) // BODY


def first_head(c):
    return 8 * (c // 4) + c % 4


def quadrant(g, i):
    return 2 * (g % 2) + i


class Step:

    def __init__(self, b, s, it):
        self.b, self.s, self.it = b, s, it
        self.par = b % 2

    def count(self, per, extra):
        v = per * self.b + extra
        assert self.it is None or v > 0
        return v if self.it is None else self.it * (2 * per) + v

    def count2(self, per, extra):
        v = per * (self.b // 2) + extra
        assert self.it is None or v > 0
        return v if self.it is None else self.it * per + v

    def seq(self):
        return self.b if self.it is None else self.it * 2 + self.b


class Slot:
    def __init__(self, t, it=None):
        self.t, self.it = t, it

    def once(self, offset):
        if (self.t - offset) % SLOTS:
            return None
        return self.chunk(offset)

    def chunk(self, offset):
        b, s = divmod(self.t - offset, SLOTS)
        if self.it is None and not 0 <= b < B:
            return None
        return Step(b, s, self.it)


def wait(eng, sem, value):
    if isinstance(value, int):
        if value > 0:
            eng.wait_ge(sem, value)
    else:
        eng.wait_ge(sem, value)


def run_slots(eng, slot):
    for t in range(LOOP_FROM):
        slot(Slot(t))
    with eng.Fori(0, LOOPS) as it:
        for t in range(BODY):
            slot(Slot(LOOP_FROM + t, it))
    for t in range(LOOP_FROM + BODY * LOOPS, LAST):
        slot(Slot(t))


def previous_use(slot, position, uses):
    for back in range(slot.t + 1):
        earlier = Slot(slot.t - back, slot.it)
        for use in sorted(uses, key=lambda u: -u[1]):
            st = earlier.once(use[0])
            if st and (back or use[1] < position):
                return st, use
    return None


def postln_layer(nc, x, Wqkv, bqkv, Wout, bout, w_gate_up, w_proj, out):
    ctx = ExitStack()
    with ctx:
        def sb(name, shape, dt=F32):
            return ctx.enter_context(nc.sbuf_tensor(name, shape, dt))

        def ps(name, shape, dt=F32):
            return ctx.enter_context(nc.psum_tensor(name, shape, dt))

        def sem(name):
            return ctx.enter_context(nc.semaphore(name))

        NGU = 2 * F // P
        wgu_raw = sb("wgu_raw", [P, NGU, D])
        wp_raw = sb("wp_raw", [P, DT, F])
        PW = 2 * D
        PG = PW // Q_GROUP
        w_bf = sb("w_bf", [P, 2, PG, Q_GROUP], BF16)
        w_abs = sb("w_abs", [P, 2, PG, Q_GROUP], BF16)
        w_sign = sb("w_sign", [P, 2, PG, Q_GROUP], BF16)
        w_hat = sb("w_hat", [P, 2, PG, Q_GROUP], BF16)
        w_sum = sb("w_sum", [P, PG])
        w_scale = sb("w_scale", [P, PG], BF16)
        w_half = sb("w_half", [P, PG], BF16)
        wguT = sb("wguT", [P, DT, 2 * F], F32R)
        wpT = sb("wpT", [P, FT, D], F32R)
        wqkv = sb("wqkv", [P, DT, D + 2 * KV])
        wqkv_p = [sb(f"wqkv_{n}", [P, DT, D + 2 * KV], F32R) for n in ("hi", "lo")]
        wv_p = sb("wv_p", [P, DT, 2, KV], F32R)
        wo = sb("wo", [P, DT, D])
        wo_p = [sb(f"wo_{n}", [P, DT, D], F32R) for n in ("hi", "lo")]
        bq = sb("bq", [P, DT])
        bq_s = sb("bq_s", [P, DT])
        bk = sb("bk", [KV, 1])
        bv = sb("bv", [P, KV])
        bo = sb("bo", [P, D])
        ident = sb("ident", [P, P])
        ident_bf = sb("ident_bf", [P, P], BF16)
        ones = sb("ones", [P, 1])
        minus_half = sb("minus_half", [P, TT])
        ln_eps = sb("ln_eps", [P, TT])

        xn = sb("xn", [P, 2, TT, D])
        xT = [sb(f"xT_{n}", [P, DT, S], F32R) for n in ("hi", "lo")]
        q_f = sb("q_f", [P, DT, S])
        q_p = sb("q_p", [P, 2, DT, S], F32R)
        k_f = sb("k_f", [KV, S])
        k_p = sb("k_p", [KV, 2, S], F32R)
        q_dram = nc.dram_tensor("q_dram", [2, 2, D, S], F32)
        k_dram = nc.dram_tensor("k_dram", [2, 2, KV, S], F32)
        SROWS = 4 * HD
        XROWS = SROWS + 2
        q_st = sb("q_st", [XROWS, 2, H, S], F32R)
        k_st = sb("k_st", [XROWS, 2, G, S], F32R)
        v_ones = sb("v_ones", [P, 2, TT, G, 2 * HD])
        v_f = sb("v_f", [P, TT, KV])
        row_max = sb("row_max", [P, 2, H * TT])
        shift_p = [[sb(f"shift{h}_{n}", [H * TT // 2, P], F32R) for n in ("hi", "lo")] for h in range(2)]
        probs = sb("probs", [P, 2, TT, 2, S])
        pv_sb = sb("pv_sb", [P, 2, S])
        den_r = sb("den_r", [P, 2 * TT * 4])
        att = sb("att", [P, TT, D])
        attT = [sb(f"attT_{n}", [P, DT, S], F32R) for n in ("hi", "lo")]
        res = sb("res", [P, 2, TT, D])
        r1 = sb("r1", [P, TT, D])
        st1 = sb("st1", [P, TT, 6])
        mv1 = sb("mv1", [P, TT, 2])
        ve1 = sb("ve1", [P, TT])
        rstd1 = sb("rstd1", [P, TT])
        x1 = sb("x1", [P, 2, TT, D])
        x1T = [sb(f"x1T_{n}", [P, 2, DT, S], F32R) for n in ("hi", "lo")]
        tanh = sb("tanh", [P, 2, S])
        gate = sb("gate", [P, 2, S])
        gated = sb("gated", [P, 2, S])
        h_f = sb("h_f", [P, 2, S])
        h_p = [sb(f"h_{n}", [P, 2, S], F32R) for n in ("hi", "lo")]
        h_sq = sb("h_sq", [P, 2, S])
        sq_sum = sb("sq_sum", [P, 2, S])
        y_sb = sb("y_sb", [P, TT, D])
        ms = sb("ms", [P, TT])
        inv = sb("inv", [P, TT])
        r2 = sb("r2", [P, TT, D])
        st2 = sb("st2", [P, TT, 6])
        mv2 = sb("mv2", [P, TT, 2])
        ve2 = sb("ve2", [P, TT])
        rstd2 = sb("rstd2", [P, TT])
        y_out = sb("y_out", [P, 2, TT, D])

        exp_ps = ps("exp_ps", [P, TT, 2 * S])
        ffn_ps = ps("ffn_ps", [P, 2, S])
        down_ps = ps("down_ps", [P, TT, D])
        pv_ps = ps("pv_ps", [P, 2, S])
        short_ps = [ps(f"short{i}_ps", [P, TT * S]) for i in range(3)]

        def short(n, name):
            return short_ps[BANK[SHORT_OFFSET.get(name, n.t) % SLOTS, name]]

        w_loaded = [sem(f"w_loaded{i}") for i in range(3)]
        consts_made, k_ones = sem("consts_made"), sem("k_ones")
        w_act, w_red, w_dve, w_tr, w_ev = sem("w_act"), sem("w_red"), sem("w_dve"), sem("w_tr"), sem("w_ev")
        w_pool = sem("w_pool")
        wo_loaded, wo_hi, wo_split = sem("wo_loaded"), sem("wo_hi"), sem("wo_split")
        w_split_hi, w_split = sem("w_split_hi"), sem("w_split")
        x_loaded = [sem(f"x_loaded{i}") for i in range(2)]
        res_loaded = [sem(f"res_loaded{i}") for i in range(2)]
        xT_made, xT_hi, xT_lo = sem("xT_made"), sem("xT_hi"), sem("xT_lo")
        q_made, q_copied, q_lo = sem("q_made"), sem("q_copied"), sem("q_lo")
        k_made, k_copied, k_lo = sem("k_made"), sem("k_copied"), sem("k_lo")
        v_made, v_biased, v_copied = sem("v_made"), sem("v_biased"), sem("v_copied")
        qk_saved = [sem(f"qk_saved{i}") for i in range(2)]
        qk_stacked = [sem(f"qk_stacked{i}") for i in range(2)]
        max_scored, max_taken = sem("max_scored"), sem("max_taken")
        shift_turned, shift_split = sem("shift_turned"), sem("shift_split")
        shift_hi = sem("shift_hi")
        shift_loaded = [sem(f"shift_loaded{i}") for i in range(2)]
        exp_scored, exp_done = sem("exp_scored"), sem("exp_done")
        pv_done, pv_copied, pv_turned = sem("pv_done"), sem("pv_copied"), sem("pv_turned")
        den_done, att_done = sem("den_done"), sem("att_done")
        att_turned, attT_hi, attT_lo = sem("att_turned"), sem("attT_hi"), sem("attT_lo")
        bout_added, o_made = sem("bout_added"), sem("o_made")
        r1_done, bn1_done, var1_done, ve1_done, rstd1_done, x1_done = (
            sem("r1_done"), sem("bn1_done"), sem("var1_done"), sem("ve1_done"), sem("rstd1_done"), sem("x1_done"))
        x1_turned, x1T_hi, x1T_lo = sem("x1_turned"), sem("x1T_hi"), sem("x1T_lo")
        ffn_made, tanh_done, gated_done, h_done = sem("ffn_made"), sem("tanh_done"), sem("gated_done"), sem("h_done")
        h_hi, h_squared, h_lo, h_summed = sem("h_hi"), sem("h_squared"), sem("h_lo"), sem("h_summed")
        down_done, y_copied, sq_summed, ms_done, inv_done = (
            sem("down_done"), sem("y_copied"), sem("sq_summed"), sem("ms_done"), sem("inv_done"))
        r2_done, bn2_done, var2_done, ve2_done, rstd2_done, y_done = (
            sem("r2_done"), sem("bn2_done"), sem("var2_done"), sem("ve2_done"), sem("rstd2_done"), sem("y_done"))
        waited, sp_waited = sem("waited"), sem("sp_waited")
        stored = [sem(f"stored{i}") for i in range(2)]

        pieces = []
        for r in range(0, NGU, 2):
            pieces.append((wgu_raw[:, r:r + 2, :], 1, [a * D + k * P for k in range(DT) for a in range(2)],
                           wguT[:, :, r * P:(r + 2) * P]))
        for k in range(0, FT, 2):
            pieces.append((wp_raw[:, :, k * P:(k + 2) * P], 2, [r * 2 * P + a * P for a in range(2) for r in range(DT)],
                           wpT[:, k:k + 2, :]))
        turn_banks = (ffn_ps, down_ps)

        def piece(n, later):
            return W_READ.index(n.t - later) if n.it is None and n.t - later in W_READ else None

        block = ctx.enter_context(nc.Block())

        @block.sync
        def _(sp):
            sp.dma_start(xn[:, 0], x[0].rearrange("(t p) d -> p t d", p=P)).then_inc(x_loaded[0], 16)
            sp.dma_start(wqkv[:], Wqkv.rearrange("(t p) n -> p t n", p=P)).then_inc(w_loaded[0], 16)
            with nc.allow_non_contiguous_dma("bias columns"):
                sp.dma_start(bq[:], bqkv[0:D].rearrange("(t p) -> p t", p=P)).then_inc(w_loaded[0], 16)
                sp.dma_start(bk[:], bqkv[D:D + KV].rearrange("(p o) -> p o", o=1)).then_inc(w_loaded[0], 16)
            sp.dma_start(bv[:], bqkv[D + KV:D + 2 * KV].partition_broadcast(P)).then_inc(w_loaded[0], 16)
            sp.dma_start(wgu_raw[:], w_gate_up.rearrange("(t p) d -> p t d", p=P)).then_inc(w_loaded[1], 16)
            sp.dma_start(wp_raw[:], w_proj.rearrange("(t p) d -> p t d", p=P)).then_inc(w_loaded[2], 16)

            def sp_wait(semaphore, value):
                wait(sp, semaphore, value)
                if not isinstance(value, int):
                    sp.sem_inc(sp_waited, 1)

            def slot(n):
                if (st := n.once(LOAD_X)) and not (st.it is None and st.b == 0):
                    sp_wait(xT_made, st.count(1, -1))
                    sp.dma_start(xn[:, st.par], x[st.seq()].rearrange("(t p) d -> p t d", p=P)
                                 ).then_inc(x_loaded[st.par], 16)
                if n.it is None and n.t == STACK_QK + 1:
                    for g in range(G):
                        for i in range(2):
                            at, row = 64 * (g // 2) + HD * quadrant(g, i), HD * (g + 4 * i)
                            sp.dma_start(wo[at:at + HD], Wout.rearrange("(h r) n -> r h n", h=2)[row:row + HD]
                                         ).then_inc(wo_loaded, 16)
                    sp.dma_start(bo[:], bout.partition_broadcast(P)).then_inc(wo_loaded, 16)
                if st := n.once(SAVE_QK):
                    sp_wait(q_lo, st.count(1, 1))
                    sp_wait(k_lo, st.count(1, 1))
                    sp_wait(qk_stacked[st.par], st.count2(128, 0))
                    sp.dma_start(q_dram[st.par].rearrange("a (m p) t -> p a m t", p=P), q_p[:].bitcast(F32)
                                 ).then_inc(qk_saved[st.par], 16)
                    sp.dma_start(k_dram[st.par].rearrange("a p t -> p a t"), k_p[:].bitcast(F32)
                                 ).then_inc(qk_saved[st.par], 16)
                for half in range(2):
                    if st := n.once(SHIFT_T[half]):
                        sp_wait(shift_split, st.count(2, half + 1))
                        for part in range(2):
                            sp.dma_start(
                                q_st[SROWS + part:SROWS + part + 1, st.par, half * H // 2:(half + 1) * H // 2, :]
                                .bitcast(F32), shift_p[half][part][:].bitcast(F32)).then_inc(shift_loaded[half], 16)
                if st := n.once(LOAD_RES):
                    sp_wait(r1_done, st.count(1, -1))
                    sp.dma_start(res[:, st.par], x[st.seq()].rearrange("(t p) d -> p t d", p=P)
                                 ).then_inc(res_loaded[st.par], 16)
                if st := n.once(STACK_QK):
                    sp_wait(qk_saved[st.par], st.count2(32, 32))
                    sp_wait(exp_scored, st.count(8, -8))
                    for c in range(4):
                        sp.dma_start(
                            k_st[c * HD:(c + 1) * HD, st.par].bitcast(F32),
                            k_dram[st.par, c % 2].rearrange("(g d) t -> d g t", d=HD)).then_inc(qk_stacked[st.par], 16)
                        sp.dma_start(
                            q_st[c * HD:(c + 1) * HD, st.par].bitcast(F32),
                            q_dram[st.par, c // 2].rearrange("(h d) t -> d h t", d=HD)
                        ).then_inc(qk_stacked[st.par], 16)
                if st := n.once(STORE):
                    sp_wait(y_done, st.count(TT, TT))
                    sp.dma_start(out[st.seq()].rearrange("(t p) d -> p t d", p=P), y_out[:, st.par]
                                 ).then_inc(stored[st.par], 16)

            run_slots(sp, slot)
            for i in range(2):
                sp.wait_ge(stored[i], 16 * B // 2)

        @block.tensor
        def _(pe):
            def products(dst, lhs, rhs, start=True, stop=True):
                pairs = list(zip(lhs, rhs))
                for i, (a, b) in enumerate(pairs):
                    last = pe.matmul(dst, a, b, start=start and i == 0, stop=stop and i == len(pairs) - 1)
                return last

            pe.wait_ge(consts_made, 3)

            def turn_weights(c):
                pe.wait_ge(w_pool, 2 * (c + 1))
                if c >= 2:
                    pe.wait_ge(w_ev, c - 1)
                flat = w_hat[:, c % 2].rearrange("p g e -> p (g e)")
                for i, at in enumerate(pieces[c][2]):
                    last = pe.transpose(turn_banks[c % 2][:].rearrange("p a b -> p (a b)").bitcast(BF16)[:, i * P:(i + 1) * P],
                                        flat[:, at:at + P], ident_bf[:])
                last.then_inc(w_tr, 1)

            released_by = {"v": (v_copied, 1, 1), "x": (xT_lo, 1, 1), "q": (q_copied, 1, 1), "shift0": (shift_split, 2, 1),
                           "shift1": (shift_split, 2, 2), "pv0": (att_done, 4, 2), "pv1": (att_done, 4, 4),
                           "att": (attT_lo, 1, 1), "o": (r1_done, 1, 1), "k": (k_copied, 1, 1), "x1": (x1T_lo, 1, 1),
                           "sq": (ms_done, 1, 1)}
            short_users = [[] for _ in short_ps]
            for (m, name), bank in BANK.items():
                if name in SHORT_OFFSET:
                    use = (SHORT_OFFSET[name], SHORT_ORDER.index(name)) + released_by[name]
                else:
                    s, i = (m - MAX0) % SLOTS, int(name[-1])
                    use = (MAX0 + s, SHORT_ORDER.index(name), max_taken, 16, 2 * s + i + 1)
                short_users[bank].append(use)

            def use_short(n, name):
                if found := previous_use(n, SHORT_ORDER.index(name), short_users[BANK[n.t % SLOTS, name]]):
                    st, (_, _, released, per, extra) = found
                    wait(pe, released, st.count(per, extra))
                return short(n, name)

            def max_scores(n, st, i):
                if i == 0:
                    wait(pe, qk_stacked[st.par], st.count2(128, 128))
                bank = use_short(n, f"max{i}")
                head = first_head(st.s) + 4 * i
                for t in range(TT):
                    last = pe.matmul(bank[:, t * S:(t + 1) * S], q_st[0:SROWS, st.par, head, t * P:(t + 1) * P],
                                     k_st[0:SROWS, st.par, st.s % 4, :], start=True, stop=True)
                last.then_inc(max_scored, 1)

            def exp_scores(st):
                wait(pe, shift_loaded[st.s // 4], st.count(32, 32))
                wait(pe, exp_done, st.count(8, st.s))
                for t in range(TT):
                    last = pe.matmul(exp_ps[:, t, :], k_st[:, st.par, st.s % 4, t * P:(t + 1) * P],
                                     q_st[:, st.par, first_head(st.s):first_head(st.s) + 5:4, :], start=True, stop=True)
                last.then_inc(exp_scored, 1)

            def gate_up(st):
                wait(pe, x1T_lo, st.count(1, 1))
                if st.it is None and st.b == 0 and st.s == 0:
                    pe.wait_ge(w_ev, len(pieces))
                wait(pe, gated_done, st.count(8, st.s))
                for half in range(2):
                    c = half * F + st.s * P
                    last = products(ffn_ps[:, half, :],
                                    [wguT[:, k, c:c + P] for k in range(DT) for _ in range(2)],
                                    [x1T[a][:, st.par, k, :] for k in range(DT) for a in range(2)])
                last.then_inc(ffn_made, 1)

            def down(st):
                wait(pe, h_lo, st.count(8, st.s + 1))
                wait(pe, h_hi, st.count(8, st.s + 1))
                if st.s == 0:
                    wait(pe, y_copied, st.count(1, 0))
                for t in range(TT):
                    for a in range(2):
                        last = pe.matmul(down_ps[:, t, :], h_p[a][:, st.s % 2, t * P:(t + 1) * P], wpT[:, st.s, :],
                                         start=(st.s == 0 and t == 0 and a == 0), stop=(st.s == FT - 1 and a == 1),
                                         skip_group_check=True)
                last.then_inc(down_done, 1)

            def times_v(st):
                wait(pe, exp_done, st.count(8, st.s + 1))
                wait(pe, v_copied, st.count(1, 1))
                if st.s % 4 == 0:
                    wait(pe, pv_copied, st.count(2, st.s // 4))
                g = st.s % 4
                for t in range(TT):
                    for i in range(2):
                        r = 32 * quadrant(g, i)
                        last = pe.matmul(pv_ps[r:r + 32, g // 2, :], v_ones[:, st.par, t, g, :],
                                         probs[:, st.s % 2, t, i, :], start=(t == 0), stop=(t == TT - 1),
                                         tile_position=(0, r))
                last.then_inc(pv_done, 1)

            def turn(bank, src, done):
                for i, blk in enumerate(src):
                    last = pe.transpose(bank[:, i * P:(i + 1) * P], blk, ident[:])
                last.then_inc(done, 1)

            def turn_maxima(bank, st, half):
                wait(pe, max_taken, st.count(16, 8 * half + 8))
                pe.transpose(bank[0:H * TT // 2, 0:P], row_max[:, st.par, half * H:(half + 1) * H], ident[:]
                             ).then_inc(shift_turned, 1)

            def slot(n):
                if st := n.chunk(FFN0):
                    gate_up(st)
                if st := n.chunk(MAX0):
                    if st.it is None and st.b == 0 and st.s == 0:
                        pe.wait_ge(k_ones, 1)
                    max_scores(n, st, 0)
                if st := n.chunk(EXP0):
                    exp_scores(st)
                if st := n.once(X1_T):
                    bank = use_short(n, "x1")
                    wait(pe, x1_done, st.count(TT, TT))
                    turn(bank, [x1[:, st.par, t, k * P:(k + 1) * P] for k in range(DT) for t in range(TT)], x1_turned)
                if st := n.once(X_T):
                    bank = use_short(n, "x")
                    wait(pe, x_loaded[st.par], st.count2(16, 16))
                    turn(bank, [xn[:, st.par, t, k * P:(k + 1) * P] for k in range(DT) for t in range(TT)], xT_made)
                if st := n.once(PROJ_V):
                    bank = use_short(n, "v")
                    wait(pe, xT_lo, st.count(1, 1))
                    for t in range(TT):
                        last = products(bank[:, t * 2 * KV:(t + 1) * 2 * KV],
                                        [xT[a][:, k, t * P:(t + 1) * P] for k in range(DT) for a in range(2)],
                                        [wv_p[:, k] for k in range(DT) for _ in range(2)])
                    last.then_inc(v_made, 1)
                if st := n.once(SHIFT_T[0]):
                    bank = use_short(n, "shift0")
                    turn_maxima(bank, st, 0)
                if st := n.once(PROJ_Q):
                    bank = use_short(n, "q")
                    wait(pe, xT_lo, st.count(1, 1))
                    wait(pe, w_split, 1)
                    for m in range(DT):
                        last = products(bank[:, m * S:(m + 1) * S],
                                        [wqkv_p[c][:, k, m * P:(m + 1) * P] for k in range(DT) for c in range(2) for _ in range(2)],
                                        [xT[a][:, k, :] for k in range(DT) for _ in range(2) for a in range(2)])
                    last.then_inc(q_made, 1)
                for half in range(2):
                    if st := n.once(PV_T[half]):
                        bank = use_short(n, f"pv{half}")
                        wait(pe, pv_copied, st.count(2, half + 1))
                        turn(bank, [pv_sb[:, g, t * P:(t + 1) * P] for g in range(2) for t in range(TT)], pv_turned)
                if st := n.chunk(MAX0):
                    max_scores(n, st, 1)
                if st := n.chunk(PV0):
                    times_v(st)
                if st := n.once(PROJ_O):
                    bank = use_short(n, "o")
                    wait(pe, attT_lo, st.count(1, 1))
                    wait(pe, wo_split, 1)
                    for t in range(TT):
                        last = products(bank[:, t * D:(t + 1) * D],
                                        [attT[a][:, m, t * P:(t + 1) * P] for m in range(DT) for a in range(2) for _ in range(2)],
                                        [wo_p[c][:, m, :] for m in range(DT) for _ in range(2) for c in range(2)])
                    last.then_inc(o_made, 1)
                if st := n.once(PROJ_K):
                    bank = use_short(n, "k")
                    last = products(bank[0:KV, 0:S],
                                    [wqkv_p[c][:, k, D:D + KV] for k in range(DT) for c in range(2) for _ in range(2)],
                                    [xT[a][:, k, :] for k in range(DT) for _ in range(2) for a in range(2)])
                    last.then_inc(k_made, 1)
                if st := n.once(ATT_T):
                    bank = use_short(n, "att")
                    wait(pe, att_done, st.count(4, 4))
                    turn(bank, [att[:, t, m * P:(m + 1) * P] for m in range(DT) for t in range(TT)], att_turned)
                if (c := piece(n, W_TURN)) is not None:
                    turn_weights(c)
                if st := n.chunk(DOWN0):
                    down(st)
                if st := n.once(SHIFT_T[1]):
                    bank = use_short(n, "shift1")
                    turn_maxima(bank, st, 1)
                if st := n.once(SUM_SQ):
                    bank = use_short(n, "sq")
                    wait(pe, h_summed, st.count(FT - 1, FT - 1))
                    for t in range(TT):
                        last = pe.matmul(bank[:, t:t + 1], sq_sum[:, st.par, t * P:(t + 1) * P], ones[:],
                                         start=True, stop=True)
                    last.then_inc(sq_summed, 1)

            run_slots(pe, slot)

        @block.scalar
        def _(act):
            act.wait_ge(w_loaded[0], 16 * 4)
            act.activation(wqkv_p[0][:], wqkv[:], ACT.Identity).then_inc(w_split_hi, 1)
            act.activation(bq_s[:], bq[:], ACT.Identity, scale=1.0 / HD).then_inc(w_split_hi, 1)
            act.activation(wv_p[:, :, 0, :], wqkv[:, :, D + KV:], ACT.Identity).then_inc(w_split_hi, 1)
            act.wait_ge(w_split_hi, 3)

            def read_weights(c):
                raw, load = pieces[c][0:2]
                act.wait_ge(w_loaded[load], 16)
                if c >= 2:
                    act.wait_ge(w_pool, 2 * (c - 1))
                flat = w_bf[:, c % 2].rearrange("p g e -> p (g e)")
                act.activation(flat.rearrange("p (a b) -> p a b", a=2), raw, ACT.Identity).then_inc(w_act, 1)
                act.wait_ge(w_act, 3 * c + 1)
                act.activation(w_abs[:, c % 2].rearrange("p g e -> p (g e)"), flat, ACT.Abs).then_inc(w_act, 1)
                act.activation(w_sign[:, c % 2].rearrange("p g e -> p (g e)"), flat, ACT.Sign).then_inc(w_act, 1)

            def high(dst, src):
                return act.activation(dst, src, ACT.Identity)

            def both(n, name):
                return short(n, name)[:].rearrange("p (k t) -> p k t", k=2)

            def slot(n):
                if st := n.chunk(FFN0):
                    wait(act, ffn_made, st.count(8, st.s + 1))
                    wait(act, h_done, st.count(8, st.s - 1))
                    act.activation(gate[:, st.s % 2, :], ffn_ps[:, 0, :], ACT.Identity)
                    act.activation(tanh[:, st.s % 2, :], ffn_ps[:, 0, :], ACT.Tanh, scale=0.5).then_inc(tanh_done, 1)
                if st := n.once(X1_HIGH):
                    wait(act, x1_turned, st.count(1, 1))
                    wait(act, ffn_made, st.count(8, -8))
                    high(x1T[0][:, st.par], both(n, "x1")).then_inc(x1T_hi, 1)
                if st := n.once(X_HIGH):
                    wait(act, xT_made, st.count(1, 1))
                    wait(act, v_made, st.count(1, 0))
                    high(xT[0][:], both(n, "x")).then_inc(xT_hi, 1)
                if st := n.chunk(EXP0):
                    wait(act, exp_scored, st.count(8, st.s + 1))
                    wait(act, pv_done, st.count(8, st.s - 1))
                    act.activation(probs[:, st.s % 2], exp_ps[:], ACT.Exp).then_inc(exp_done, 1)
                if st := n.once(ATT_HIGH):
                    wait(act, att_turned, st.count(1, 1))
                    wait(act, o_made, st.count(1, 0))
                    high(attT[0][:], both(n, "att")).then_inc(attT_hi, 1)
                if st := n.once(Q_COPY):
                    wait(act, q_made, st.count(1, 1))
                    wait(act, q_lo, st.count(1, 0))
                    if st.it is not None or st.b > 0:
                        wait(act, qk_saved[1 - st.par], Step(st.b - 1, 0, st.it).count2(32, 32))
                    for m in range(DT):
                        for dst in (q_f[:, m, :], q_p[:, 0, m, :]):
                            last = act.activation(dst, short(n, "q")[:, m * S:(m + 1) * S], ACT.Identity,
                                                  bias=bq_s[:, m:m + 1], scale=1.0 / HD)
                    last.then_inc(q_copied, 1)
                for half in range(2):
                    if st := n.once(PV_COPY[half]):
                        wait(act, pv_done, st.count(8, 4 * half + 4))
                        wait(act, pv_turned, st.count(2, half))
                        act.activation(pv_sb[:], pv_ps[:], ACT.Identity).then_inc(pv_copied, 1)
                if st := n.chunk(H_HIGH0):
                    wait(act, h_done, st.count(8, st.s + 1))
                    wait(act, down_done, st.count(8, st.s - 1))
                    high(h_p[0][:, st.s % 2, :], h_f[:, st.s % 2, :]).then_inc(h_hi, 1)
                    if st.s == 0:
                        wait(act, sq_summed, st.count(1, -1))
                        dst = sq_sum[:, st.par, :]
                    else:
                        wait(act, h_summed, st.count(FT - 1, max(st.s - 2, 0)))
                        dst = h_sq[:, st.s % 2, :]
                    act.activation(dst, h_f[:, st.s % 2, :], ACT.Square).then_inc(h_squared, 1)
                if st := n.once(K_COPY):
                    wait(act, k_made, st.count(1, 1))
                    wait(act, k_lo, st.count(1, 0))
                    for dst in (k_f[:], k_p[:, 0, :]):
                        last = act.activation(dst, short(n, "k")[0:KV, 0:S], ACT.Identity, bias=bk[:, 0:1])
                    last.then_inc(k_copied, 1)
                if st := n.once(Y_COPY):
                    wait(act, down_done, st.count(8, 8))
                    wait(act, r2_done, st.count(TT, 0))
                    act.activation(y_sb[:], down_ps[:], ACT.Identity).then_inc(y_copied, 1)
                if (c := piece(n, W_PLACE)) is not None:
                    act.wait_ge(w_tr, c + 1)
                    high(pieces[c][3], turn_banks[c % 2][:].rearrange("p a b -> p (a b)").bitcast(BF16)[:, 0:4 * P]
                         .rearrange("p (k t) -> p k t", k=2)).then_inc(w_ev, 1)
                if (c := piece(n, 0)) is not None:
                    read_weights(c)
                if n.it is None and n.t == WO_SPLIT:
                    act.wait_ge(wo_loaded, 16 * (2 * G + 1))
                    act.activation(wo_p[0][:], wo[:], ACT.Identity).then_inc(wo_hi, 1)

            run_slots(act, slot)

        @block.vector
        def _(dve):
            dve.memset(k_st[SROWS:XROWS].bitcast(F32), 1.0).then_inc(k_ones, 1)
            dve.wait_ge(w_split_hi, 3)
            dve.tensor_tensor(wqkv_p[1][:], wqkv[:], wqkv_p[0][:].bitcast(F32), ALU.subtract)
            dve.tensor_tensor(wv_p[:, :, 1, :], wqkv[:, :, D + KV:], wqkv_p[0][:, :, D + KV:].bitcast(F32), ALU.subtract
                              ).then_inc(w_split, 1)

            def low(dst, src, hi):
                return dve.tensor_tensor(dst, src, hi.bitcast(F32), ALU.subtract)

            def both(n, name):
                return short(n, name)[:].rearrange("p (k t) -> p k t", k=2)

            def take_maximum(n, st, i):
                wait(dve, max_scored, st.count(16, 2 * st.s + i + 1))
                if st.s == 0 and i == 0:
                    wait(dve, shift_turned, st.count(2, -2))
                head = first_head(st.s) + 4 * i
                dve.tensor_reduce(row_max[:, st.par, head * TT:(head + 1) * TT], short(n, f"max{i}")[:].rearrange("p (t k) -> p t k", t=TT), AX.X, ALU.max
                                  ).then_inc(max_taken, 1)

            def shift_rows(n, st, half):
                src = short(n, f"shift{half}")[0:H * TT // 2, 0:P]
                hi, lo = shift_p[half]
                wait(dve, shift_turned, st.count(2, half + 1))
                wait(dve, shift_loaded[half], st.count(32, 0))
                dve.tensor_scalar(hi[:], src, -1.0, None, ALU.mult).then_inc(shift_hi, 1)
                wait(dve, shift_hi, st.count(2, half + 1))
                dve.scalar_tensor_tensor(lo[:], src, -1.0, hi[:].bitcast(F32), ALU.mult, ALU.subtract
                                         ).then_inc(shift_split, 1)

            def tern_weights(c):
                dve.wait_ge(w_act, 3 * c + 3)
                dve.tensor_reduce(w_sum[:], w_abs[:, c % 2], AX.X, ALU.add).then_inc(w_red, 1)
                dve.wait_ge(w_red, 3 * c + 1)
                dve.tensor_scalar(w_scale[:], w_sum[:], 1.0 / Q_GROUP, 1e-8, ALU.mult, ALU.max).then_inc(w_red, 1)
                dve.wait_ge(w_red, 3 * c + 2)
                dve.tensor_scalar(w_half[:], w_scale[:], 0.5, None, ALU.mult).then_inc(w_red, 1)
                dve.wait_ge(w_red, 3 * c + 3)
                if c >= 2:
                    dve.wait_ge(w_tr, c - 1)
                half = w_half[:].unsqueeze(2).broadcast_to([P, PG, Q_GROUP])
                scale = w_scale[:].unsqueeze(2).broadcast_to([P, PG, Q_GROUP])
                hat = w_hat[:, c % 2]
                for i, (a, b, op) in enumerate(((w_abs[:, c % 2], half, ALU.is_gt), (hat, scale, ALU.mult),
                                                (hat, w_sign[:, c % 2], ALU.mult))):
                    if i:
                        dve.wait_ge(w_dve, 3 * c + i)
                    dve.tensor_tensor(hat, a, b, op).then_inc(w_dve, 1)

            def slot(n):
                if st := n.chunk(MAX0):
                    take_maximum(n, st, 0)
                if st := n.once(X_LOW):
                    wait(dve, xT_hi, st.count(1, 1))
                    low(xT[1][:], both(n, "x"), xT[0][:]).then_inc(xT_lo, 1)
                if st := n.chunk(GATE0):
                    wait(dve, tanh_done, st.count(8, st.s + 1))
                    dve.scalar_tensor_tensor(gated[:, st.s % 2, :], tanh[:, st.s % 2, :], 1.0, ffn_ps[:, 1, :],
                                             ALU.add, ALU.mult).then_inc(gated_done, 1)
                if st := n.chunk(H0):
                    wait(dve, gated_done, st.count(8, st.s + 1))
                    wait(dve, h_lo, st.count(8, st.s - 1))
                    wait(dve, h_squared, st.count(8, st.s - 1))
                    dve.tensor_tensor(h_f[:, st.s % 2, :], gated[:, st.s % 2, :], gate[:, st.s % 2, :], ALU.mult
                                      ).then_inc(h_done, 1)
                if st := n.once(X1_LOW):
                    wait(dve, x1T_hi, st.count(1, 1))
                    low(x1T[1][:, st.par], both(n, "x1"), x1T[0][:, st.par]).then_inc(x1T_lo, 1)
                if st := n.once(SHIFT_SPLIT[0]):
                    shift_rows(n, st, 0)
                if st := n.once(LN2_STATS):
                    wait(dve, inv_done, st.count(1, 1))
                    wait(dve, y_copied, st.count(1, 1))
                    for t in range(TT):
                        dve.scalar_tensor_tensor(r2[:, t, :], y_sb[:, t, :], inv[:, t:t + 1], x1[:, st.par, t, :],
                                                 ALU.mult, ALU.add).then_inc(r2_done, 1)
                    for t in range(TT):
                        wait(dve, r2_done, st.count(TT, t + 1))
                        dve.bn_stats(st2[:, t, :], r2[:, t, :]).then_inc(bn2_done, 1)
                    wait(dve, bn2_done, st.count(TT, TT))
                    dve.sem_inc(waited, 1)
                    for t in range(TT):
                        dve.bn_aggr(mv2[:, t, :], st2[:, t, :]).then_inc(var2_done, 1)
                if st := n.chunk(MAX0):
                    take_maximum(n, st, 1)
                if st := n.once(MEAN_SQ):
                    wait(dve, sq_summed, st.count(1, 1))
                    dve.tensor_scalar(ms[:], short(n, "sq")[:, 0:TT], 1.0 / F, 4.0 * RMS_EPS, ALU.mult, ALU.add
                                      ).then_inc(ms_done, 1)
                for half in range(2):
                    if st := n.once(PV_DIVIDE[half]):
                        pv = short(n, f"pv{half}")[:].rearrange("p (g t j e) -> p g t j e", g=2, t=TT, j=4)
                        rec = den_r[:].rearrange("p (g t j) -> p g t j", g=2, t=TT)
                        wait(dve, pv_turned, st.count(2, half + 1))
                        wait(dve, att_done, st.count(4, 2 * half))
                        dve.reciprocal(rec.rearrange("p g t j -> p (g t) j"),
                                       pv.rearrange("p g t j e -> p (g t) j e")[:, :, :, HD]).then_inc(den_done, 1)
                        wait(dve, den_done, st.count(2, half + 1))
                        if half == 0:
                            wait(dve, att_turned, st.count(1, 0))
                        for i in range(2):
                            dve.tensor_tensor(
                                att[:].rearrange("p t (h i j d) -> p t h i j d", h=2, i=2, j=4)[:, :, half, i],
                                pv[:, i, :, :, 0:HD],
                                rec[:, i].unsqueeze(3).broadcast_to([P, TT, 4, HD]), ALU.mult).then_inc(att_done, 1)
                if st := n.once(V_COPY):
                    wait(dve, v_made, st.count(1, 1))
                    v = short(n, "v")[:, 0:TT * 2 * KV].rearrange("p (t c n) -> p t c n", t=TT, c=2)
                    for t in range(TT):
                        dve.tensor_tensor(v_f[:, t, :], v[:, t, 0, :], bv[:], ALU.add).then_inc(v_biased, 1)
                    wait(dve, v_biased, st.count(TT, TT))
                    wait(dve, pv_done, st.count(8, -8))
                    for t in range(TT):
                        last = dve.tensor_tensor(
                            v_ones[:, st.par, t, :, 0:HD], v_f[:, t, :].rearrange("p (g d) -> p g d", g=G),
                            v[:, t, 1, :].rearrange("p (g d) -> p g d", g=G), ALU.add)
                    last.then_inc(v_copied, 1)
                if st := n.once(LN1_APPLY):
                    wait(dve, rstd1_done, st.count(1, 1))
                    for t in range(TT):
                        dve.tensor_scalar(x1[:, st.par, t, :], r1[:, t, :], mv1[:, t, 0:1], rstd1[:, t:t + 1],
                                          ALU.subtract, ALU.mult).then_inc(x1_done, 1)
                if st := n.once(ATT_LOW):
                    wait(dve, attT_hi, st.count(1, 1))
                    low(attT[1][:], both(n, "att"), attT[0][:]).then_inc(attT_lo, 1)
                if st := n.once(SHIFT_SPLIT[1]):
                    shift_rows(n, st, 1)
                if (c := piece(n, W_MAKE)) is not None:
                    tern_weights(c)
                if st := n.once(LN2_APPLY):
                    wait(dve, rstd2_done, st.count(1, 1))
                    wait(dve, stored[st.par], st.count2(16, 0))
                    for t in range(TT):
                        dve.tensor_scalar(y_out[:, st.par, t, :], r2[:, t, :], mv2[:, t, 0:1], rstd2[:, t:t + 1],
                                          ALU.subtract, ALU.mult).then_inc(y_done, 1)
                if st := n.once(O_ADD):
                    wait(dve, o_made, st.count(1, 1))
                    wait(dve, bout_added, st.count(1, 1))
                    dve.tensor_tensor(r1[:], both(n, "o"), res[:, st.par], ALU.add).then_inc(r1_done, 1)
                    wait(dve, r1_done, st.count(1, 1))
                    for t in range(TT):
                        dve.bn_stats(st1[:, t, :], r1[:, t, :]).then_inc(bn1_done, 1)
                    wait(dve, bn1_done, st.count(TT, TT))
                    dve.sem_inc(waited, 1)
                    for t in range(TT):
                        dve.bn_aggr(mv1[:, t, :], st1[:, t, :]).then_inc(var1_done, 1)
                if n.it is None and n.t == WO_SPLIT:
                    dve.wait_ge(wo_hi, 1)
                    dve.tensor_tensor(wo_p[1][:], wo[:], wo_p[0][:].bitcast(F32), ALU.subtract).then_inc(wo_split, 1)
                if st := n.once(K_LOW):
                    wait(dve, k_copied, st.count(1, 1))
                    low(k_p[:, 1, :], k_f[:], k_p[:, 0, :]).then_inc(k_lo, 1)

            run_slots(dve, slot)

        @block.gpsimd
        def _(pool):
            pool.memset(ident[:], 0.0).then_inc(consts_made, 1)
            pool.memset(ones[:], 1.0)
            pool.memset(minus_half[:], -0.5)
            pool.memset(ln_eps[:], LN_EPS)
            pool.memset(v_ones[:], 1.0)
            pool.wait_ge(consts_made, 1)
            pool.affine_select(out=ident[:], in_=ident[:], compare_op=ALU.not_equal, fill=1.0, base=0,
                               pattern=[[-1, P]], channel_multiplier=1).then_inc(consts_made, 1)
            pool.wait_ge(consts_made, 2)
            pool.tensor_copy(ident_bf[:], ident[:]).then_inc(consts_made, 1)

            def rsqrt(dst, src, done):
                pool.tensor_tensor(dst, src, minus_half[:], ALU.pow).then_inc(done, 1)

            def slot(n):
                if st := n.chunk(H_LOW0):
                    wait(pool, h_hi, st.count(8, st.s + 1))
                    wait(pool, down_done, st.count(8, st.s - 1))
                    pool.tensor_tensor(h_p[1][:, st.s % 2, :], h_f[:, st.s % 2, :],
                                       h_p[0][:, st.s % 2, :].bitcast(F32), ALU.subtract).then_inc(h_lo, 1)
                    if st.s:
                        wait(pool, h_squared, st.count(8, st.s + 1))
                        wait(pool, h_summed, st.count(FT - 1, st.s - 1))
                        pool.tensor_tensor(sq_sum[:, st.par, :], sq_sum[:, st.par, :], h_sq[:, st.s % 2, :], ALU.add
                                           ).then_inc(h_summed, 1)
                if st := n.once(RSTD1):
                    wait(pool, var1_done, st.count(TT, TT))
                    pool.tensor_tensor(ve1[:], mv1[:, :, 1], ln_eps[:], ALU.add).then_inc(ve1_done, 1)
                    wait(pool, ve1_done, st.count(1, 1))
                    rsqrt(rstd1[:], ve1[:], rstd1_done)
                if st := n.once(ADD_BOUT):
                    if st.it is None and st.b == 0:
                        pool.wait_ge(wo_loaded, 16 * (2 * G + 1))
                    wait(pool, res_loaded[st.par], st.count2(16, 16))
                    for t in range(TT):
                        last = pool.tensor_tensor(res[:, st.par, t, :], res[:, st.par, t, :], bo[:], ALU.add)
                    last.then_inc(bout_added, 1)
                if st := n.once(Q_LOW):
                    wait(pool, q_copied, st.count(1, 1))
                    pool.tensor_tensor(q_p[:, 1], q_f[:], q_p[:, 0].bitcast(F32), ALU.subtract).then_inc(q_lo, 1)
                if (c := piece(n, W_MAKE)) is not None:
                    pool.wait_ge(w_dve, 3 * (c + 1))
                    hat = w_hat[:, c % 2]
                    pool.tensor_tensor(hat, hat, w_bf[:, c % 2], ALU.subtract).then_inc(w_pool, 1)
                    pool.wait_ge(w_pool, 2 * c + 1)
                    pool.tensor_tensor(hat, hat, w_bf[:, c % 2], ALU.add).then_inc(w_pool, 1)
                if st := n.once(INV):
                    wait(pool, ms_done, st.count(1, 1))
                    rsqrt(inv[:], ms[:], inv_done)
                if st := n.once(RSTD2):
                    wait(pool, var2_done, st.count(TT, TT))
                    pool.tensor_tensor(ve2[:], mv2[:, :, 1], ln_eps[:], ALU.add).then_inc(ve2_done, 1)
                    wait(pool, ve2_done, st.count(1, 1))
                    rsqrt(rstd2[:], ve2[:], rstd2_done)

            run_slots(pool, slot)


_INS = ["L0_attn_x", "L0_attn_Wqkv", "L0_attn_bqkv", "L0_attn_Wout", "L0_attn_bout", "L0_ffn_w_gate_up",
        "L0_ffn_w_proj"]


def kernel(**inputs):
    import numpy as _np
    import concourse.bacc as _bacc
    from concourse import mybir as _mybir
    from concourse.bass_utils import run_bass_kernel_spmd as _run

    nc = _bacc.Bacc("TRN2", target_bir_lowering=False, num_devices=1)
    arrays, args = {}, []
    for name in _INS:
        a = _np.ascontiguousarray(inputs[name])
        arrays[f"in_{name}_dram"] = a
        args.append(nc.dram_tensor(f"in_{name}_dram", a.shape, _mybir.dt.from_np(a.dtype), kind="ExternalInput").ap())
    out = nc.dram_tensor("out_0_dram", (B, S, D), _mybir.dt.float32, kind="ExternalOutput").ap()
    postln_layer(nc, *args, out)
    r = _run(nc, [arrays], core_ids=[0])
    return r.results[0]["out_0_dram"]
```
